# Optimizing a Trainium2 kernel written in Bass

```python
import numpy as np
import jax
import jax.numpy as jnp

def _softmax(x, axis=-1):
    return jax.nn.softmax(x, axis=axis)

def _gelu(x):
    return jax.nn.gelu(x, approximate=True)

def _silu(x):
    return jax.nn.silu(x)

def _sigmoid(x):
    return jax.nn.sigmoid(x)

def _layernorm(x, axis=-1, eps=1e-05):
    m = jnp.mean(x, axis=axis, keepdims=True)
    v = jnp.var(x, axis=axis, keepdims=True)
    return (x - m) / jnp.sqrt(v + eps)

def _scatter_add(tgt, idx, src, axis=0):
    return tgt.at[idx].add(src)

def _segment_sum(src, seg, n):
    return jax.ops.segment_sum(src, seg, n)
kernel_name = 'mk_adaln_d1_jaxref_r8_91831e'

def setup_inputs(seed: int=0):
    np.random.seed(seed)
    _w = jnp.asarray

    def _L0_attn_setup():
        import jax, jax.numpy as jnp
        import numpy as np
        B, N, D = (4, 512, 128)
        H, DH = (16, 64)
        DFF = 512
        M = 64
        EPS_KERN = 1e-06
        EPS_LN = 1e-06

        def _softmax_kernel_feats(data, proj, is_query):
            dn = 1.0 / jnp.sqrt(jnp.sqrt(jnp.float32(data.shape[-1])))
            ratio = 1.0 / jnp.sqrt(jnp.float32(proj.shape[0]))
            data_dash = jnp.einsum('bnhd,md->bnhm', data * dn, proj)
            diag = jnp.sum(jnp.square(data), axis=-1, keepdims=True) * (dn * dn) / 2.0
            if is_query:
                mx = jnp.max(data_dash, axis=-1, keepdims=True)
            else:
                mx = jnp.max(data_dash)
            return ratio * (jnp.exp(data_dash - diag - mx) + EPS_KERN)

        def _layernorm(x, g, b):
            mu = jnp.mean(x, axis=-1, keepdims=True)
            var = jnp.mean(jnp.square(x - mu), axis=-1, keepdims=True)
            return (x - mu) * jax.lax.rsqrt(var + EPS_LN) * g + b

        def _encoder_forward(x, Wq, Wk, Wv, Wo, proj, W1, b1, W2, b2, ln1_g, ln1_b, ln2_g, ln2_b):
            q = jnp.einsum('bnd,dhk->bnhk', x, Wq)
            k = jnp.einsum('bnd,dhk->bnhk', x, Wk)
            v = jnp.einsum('bnd,dhk->bnhk', x, Wv)
            qf = _softmax_kernel_feats(q, proj, True)
            kf = _softmax_kernel_feats(k, proj, False)
            kv = jnp.einsum('bnhm,bnhd->bhmd', kf, v)
            num = jnp.einsum('bnhm,bhmd->bnhd', qf, kv)
            den = jnp.einsum('bnhm,bhm->bnh', qf, jnp.sum(kf, axis=1))
            attn = num / den[..., None]
            attn_out = jnp.einsum('bnhd,hdo->bno', attn, Wo)
            out1 = _layernorm(x + attn_out, ln1_g, ln1_b)
            h = jax.nn.elu(out1 @ W1 + b1)
            ffn_out = h @ W2 + b2
            return _layernorm(out1 + ffn_out, ln2_g, ln2_b)
        key = jax.random.key(seed)
        ks = jax.random.split(key, 12)
        s = 0.02
        inp = {'x': jax.random.normal(ks[0], (B, N, D), jnp.float32), 'Wq': jax.random.normal(ks[1], (D, H, DH), jnp.float32) * s, 'Wk': jax.random.normal(ks[2], (D, H, DH), jnp.float32) * s, 'Wv': jax.random.normal(ks[3], (D, H, DH), jnp.float32) * s, 'Wo': jax.random.normal(ks[4], (H, DH, D), jnp.float32) * s, 'proj': jax.random.normal(ks[5], (M, DH), jnp.float32), 'W1': jax.random.normal(ks[6], (D, DFF), jnp.float32) * s, 'b1': jnp.zeros((DFF,), jnp.float32), 'W2': jax.random.normal(ks[7], (DFF, D), jnp.float32) * s, 'b2': jnp.zeros((D,), jnp.float32), 'ln1_g': jnp.ones((D,), jnp.float32), 'ln1_b': jnp.zeros((D,), jnp.float32), 'ln2_g': jnp.ones((D,), jnp.float32), 'ln2_b': jnp.zeros((D,), jnp.float32)}
        return inp
    _L0_attn_in = _L0_attn_setup()

    def _L0_ffn_setup():
        import jax, jax.numpy as jnp
        import numpy as np
        H = 8
        KD = 128
        TOPK = 8
        NUM_KEYS = 32
        N_EXPERTS = NUM_KEYS * NUM_KEYS
        N_DIM = 128
        BN_EPS = 1e-05

        def gelu_new(x):
            c = jnp.sqrt(jnp.asarray(2.0 / jnp.pi, x.dtype))
            return 0.5 * x * (1.0 + jnp.tanh(c * (x + 0.044715 * x * x * x)))
        key = jax.random.key(seed)
        ks = jax.random.split(key, 5)
        b, s = (2, 128)
        x = jax.random.normal(ks[0], (b, s, N_DIM), dtype=jnp.float32)
        w_q = jax.random.normal(ks[1], (N_DIM, 2 * H * KD), dtype=jnp.float32) * 0.02
        bn_gamma = jnp.ones((2 * H * KD,), dtype=jnp.float32)
        bn_beta = jnp.zeros((2 * H * KD,), dtype=jnp.float32)
        keys = jax.random.normal(ks[2], (H, NUM_KEYS, 2, KD), dtype=jnp.float32) * 0.02
        down_embed = jax.random.normal(ks[3], (N_EXPERTS, N_DIM), dtype=jnp.float32) * 0.02
        up_embed = jax.random.normal(ks[4], (N_EXPERTS, N_DIM), dtype=jnp.float32) * 0.02
        return {'x': x, 'w_q': w_q, 'bn_gamma': bn_gamma, 'bn_beta': bn_beta, 'keys': keys, 'down_embed': down_embed, 'up_embed': up_embed}
    _L0_ffn_in = _L0_ffn_setup()
    _L0_c = _w((lambda *s: np.random.randn(*s).astype(np.float32) * 0.05)(16, 128))
    _L0_wmod = _w((lambda *s: np.random.randn(*s).astype(np.float32) * 0.05)(128, 6 * 128) * 128 ** (-0.5))
    _d = {'L0_attn_x': _L0_attn_in['x'], 'L0_attn_Wq': _L0_attn_in['Wq'], 'L0_attn_Wk': _L0_attn_in['Wk'], 'L0_attn_Wv': _L0_attn_in['Wv'], 'L0_attn_Wo': _L0_attn_in['Wo'], 'L0_attn_proj': _L0_attn_in['proj'], 'L0_attn_W1': _L0_attn_in['W1'], 'L0_attn_b1': _L0_attn_in['b1'], 'L0_attn_W2': _L0_attn_in['W2'], 'L0_attn_b2': _L0_attn_in['b2'], 'L0_attn_ln1_g': _L0_attn_in['ln1_g'], 'L0_attn_ln1_b': _L0_attn_in['ln1_b'], 'L0_attn_ln2_g': _L0_attn_in['ln2_g'], 'L0_attn_ln2_b': _L0_attn_in['ln2_b'], 'L0_ffn_w_q': _L0_ffn_in['w_q'], 'L0_ffn_bn_gamma': _L0_ffn_in['bn_gamma'], 'L0_ffn_bn_beta': _L0_ffn_in['bn_beta'], 'L0_ffn_keys': _L0_ffn_in['keys'], 'L0_ffn_down_embed': _L0_ffn_in['down_embed'], 'L0_ffn_up_embed': _L0_ffn_in['up_embed'], 'L0_c': _L0_c, 'L0_wmod': _L0_wmod}
    _x0 = _d['L0_attn_x']
    _d['L0_attn_x'] = jax.random.normal(jax.random.fold_in(jax.random.key(seed), 1), (16, 256, 128), dtype=_x0.dtype)
    del _x0
    return _d

def reference(L0_attn_x, L0_attn_Wq, L0_attn_Wk, L0_attn_Wv, L0_attn_Wo, L0_attn_proj, L0_attn_W1, L0_attn_b1, L0_attn_W2, L0_attn_b2, L0_attn_ln1_g, L0_attn_ln1_b, L0_attn_ln2_g, L0_attn_ln2_b, L0_ffn_w_q, L0_ffn_bn_gamma, L0_ffn_bn_beta, L0_ffn_keys, L0_ffn_down_embed, L0_ffn_up_embed, L0_c, L0_wmod):

    def _L0_attn_ref(x, Wq, Wk, Wv, Wo, proj, W1, b1, W2, b2, ln1_g, ln1_b, ln2_g, ln2_b):
        import jax, jax.numpy as jnp
        import numpy as np
        B, N, D = (4, 512, 128)
        H, DH = (16, 64)
        DFF = 512
        M = 64
        EPS_KERN = 1e-06
        EPS_LN = 1e-06

        def _softmax_kernel_feats(data, proj, is_query):
            dn = 1.0 / jnp.sqrt(jnp.sqrt(jnp.float32(data.shape[-1])))
            ratio = 1.0 / jnp.sqrt(jnp.float32(proj.shape[0]))
            data_dash = jnp.einsum('bnhd,md->bnhm', data * dn, proj)
            diag = jnp.sum(jnp.square(data), axis=-1, keepdims=True) * (dn * dn) / 2.0
            if is_query:
                mx = jnp.max(data_dash, axis=-1, keepdims=True)
            else:
                mx = jnp.max(data_dash)
            return ratio * (jnp.exp(data_dash - diag - mx) + EPS_KERN)

        def _layernorm(x, g, b):
            mu = jnp.mean(x, axis=-1, keepdims=True)
            var = jnp.mean(jnp.square(x - mu), axis=-1, keepdims=True)
            return (x - mu) * jax.lax.rsqrt(var + EPS_LN) * g + b

        def _encoder_forward(x, Wq, Wk, Wv, Wo, proj, W1, b1, W2, b2, ln1_g, ln1_b, ln2_g, ln2_b):
            q = jnp.einsum('bnd,dhk->bnhk', x, Wq)
            k = jnp.einsum('bnd,dhk->bnhk', x, Wk)
            v = jnp.einsum('bnd,dhk->bnhk', x, Wv)
            qf = _softmax_kernel_feats(q, proj, True)
            kf = _softmax_kernel_feats(k, proj, False)
            kv = jnp.einsum('bnhm,bnhd->bhmd', kf, v)
            num = jnp.einsum('bnhm,bhmd->bnhd', qf, kv)
            den = jnp.einsum('bnhm,bhm->bnh', qf, jnp.sum(kf, axis=1))
            attn = num / den[..., None]
            attn_out = jnp.einsum('bnhd,hdo->bno', attn, Wo)
            out1 = _layernorm(x + attn_out, ln1_g, ln1_b)
            h = jax.nn.elu(out1 @ W1 + b1)
            ffn_out = h @ W2 + b2
            return _layernorm(out1 + ffn_out, ln2_g, ln2_b)
        return _encoder_forward(x, Wq, Wk, Wv, Wo, proj, W1, b1, W2, b2, ln1_g, ln1_b, ln2_g, ln2_b)

    def _L0_ffn_ref(x, w_q, bn_gamma, bn_beta, keys, down_embed, up_embed):
        import jax, jax.numpy as jnp
        import numpy as np
        H = 8
        KD = 128
        TOPK = 8
        NUM_KEYS = 32
        N_EXPERTS = NUM_KEYS * NUM_KEYS
        N_DIM = 128
        BN_EPS = 1e-05

        def gelu_new(x):
            c = jnp.sqrt(jnp.asarray(2.0 / jnp.pi, x.dtype))
            return 0.5 * x * (1.0 + jnp.tanh(c * (x + 0.044715 * x * x * x)))
        b, n, d = x.shape
        q = jnp.einsum('bnd,de->bne', x, w_q)
        mean = jnp.mean(q, axis=(0, 1))
        var = jnp.var(q, axis=(0, 1))
        q = (q - mean) * jax.lax.rsqrt(var + BN_EPS) * bn_gamma + bn_beta
        q = q.reshape(b, n, 2, H, KD).transpose(2, 0, 1, 3, 4)
        sim = jnp.einsum('pbnhd,hkpd->pbnhk', q, keys)
        sx, ix = jax.lax.top_k(sim[0], TOPK)
        sy, iy = jax.lax.top_k(sim[1], TOPK)
        all_scores = (sx[..., :, None] + sy[..., None, :]).reshape(b, n, H, TOPK * TOPK)
        all_indices = (ix[..., :, None] * NUM_KEYS + iy[..., None, :]).reshape(b, n, H, TOPK * TOPK)
        scores, pk = jax.lax.top_k(all_scores, TOPK)
        indices = jnp.take_along_axis(all_indices, pk, axis=-1)
        wd = down_embed[indices]
        wu = up_embed[indices]
        h = jnp.einsum('bnd,bnhkd->bnhk', x, wd)
        h = gelu_new(h)
        h = jax.nn.softmax(scores, axis=-1) * h
        out = jnp.einsum('bnhk,bnhkd->bnd', h, wu)
        return out
    x = L0_attn_x
    mod = (_silu(L0_c) @ L0_wmod).reshape(L0_c.shape[0], 6, 1, -1)
    sa, ca, ga, sb, cb, gb = (mod[:, 0], mod[:, 1], mod[:, 2], mod[:, 3], mod[:, 4], mod[:, 5])
    ga = (2 * (ga >= 0) - 1) * jnp.maximum(jnp.abs(ga), 0.25)
    gb = (2 * (gb >= 0) - 1) * jnp.maximum(jnp.abs(gb), 0.25)
    h = _layernorm(x, axis=-1) * (1 + ca) + sa
    x = x + ga * _L0_attn_ref(h, L0_attn_Wq, L0_attn_Wk, L0_attn_Wv, L0_attn_Wo, L0_attn_proj, L0_attn_W1, L0_attn_b1, L0_attn_W2, L0_attn_b2, L0_attn_ln1_g, L0_attn_ln1_b, L0_attn_ln2_g, L0_attn_ln2_b)
    h = _layernorm(x, axis=-1) * (1 + cb) + sb
    x = x + gb * _L0_ffn_ref(h, L0_ffn_w_q, L0_ffn_bn_gamma, L0_ffn_bn_beta, L0_ffn_keys, L0_ffn_down_embed, L0_ffn_up_embed)
    return x

_drawn_inputs = setup_inputs


def setup_inputs(seed=0):
    import zlib

    import numpy as np

    out = dict(_drawn_inputs(seed))
    spreads = {'L0_attn_b1': (0.0, 0.8),
     'L0_attn_b2': (0.0, 0.308),
     'L0_attn_ln1_g': (1.0, 0.2),
     'L0_attn_ln1_b': (0.0, 0.331),
     'L0_attn_ln2_g': (1.0, 0.2),
     'L0_attn_ln2_b': (0.0, 0.294),
     'L0_ffn_bn_gamma': (1.0, 0.6),
     'L0_ffn_bn_beta': (0.0, 0.8)}
    factors = {'L0_attn_Wq': 64.0,
     'L0_attn_Wk': 64.0,
     'L0_attn_Wv': 8.0,
     'L0_attn_Wo': 8.0,
     'L0_attn_proj': 64.0,
     'L0_ffn_w_q': 8.0,
     'L0_ffn_keys': 8.0,
     'L0_ffn_down_embed': 8.0,
     'L0_ffn_up_embed': 8.0,
     'L0_attn_W1': 2.925}
    for name, (base, spread) in spreads.items():
        noise = np.random.default_rng([zlib.crc32(name.encode()), seed]).standard_normal(out[name].shape)
        drawn = base * np.exp(spread * noise) if base else spread * noise
        out[name] = jnp.asarray(drawn.astype(out[name].dtype))
    for name, factor in factors.items():
        out[name] = (out[name] * factor).astype(out[name].dtype)
    return out
```

```python
from contextlib import ExitStack

import concourse.bass as bass
from concourse import mybir

F32 = mybir.dt.float32
F16 = mybir.dt.float16
U16 = mybir.dt.uint16
U32 = mybir.dt.uint32
ALU = mybir.AluOpType
ACT = mybir.ActivationFunctionType
AX = mybir.AxisListType
ADD, SUB, MUL, MAX, MIN = ALU.add, ALU.subtract, ALU.mult, ALU.max, ALU.min

P = 128
BATCH, SEQ, D = 16, 256, 128
JT = SEQ // P
TILES = BATCH * JT
HEADS, DH, M = 16, 64, 64
HM = HEADS * M
PAIRS = HEADS // 2
DFF = 512
FC = DFF // P
EPS_KERN = 1e-6
EPS_LN_ATTN, EPS_LN, EPS_BN = 1e-6, 1e-5, 1e-5
DN = float(DH) ** -0.25
PH, NK, TOPK = 8, 32, 8
NE = NK * NK
EB = NE // P
QB = 2 * PH
RANKS = [TOPK // (a + 1) for a in range(TOPK)]
CAND = sum(RANKS)
PAIR = PH * TOPK
KEYB = 8192.0
HALF = P // 2
WSCALE = 2048.0
RND = 12582912.0

SA, CA1, GAG, GAB, SB, CB1, GB = range(7)
NV = 8


def sweep(eng, n, lag, body):
    head = (lag + 3) // 2 * 2
    end = head + (n - head) // 2 * 2
    for it in range(head):
        body(it, it % 2, it // 2)
    with eng.Fori(head // 2, end // 2) as pair:
        body(pair * 2, 0, pair)
        body(pair * 2 + 1, 1, pair)
    for it in range(end, n + lag):
        body(it, it % 2, it // 2)


def inside(idx, n):
    return not isinstance(idx, int) or 0 <= idx < n


def wait_free(eng, sem, idx, per=1, depth=2):
    if isinstance(idx, int) and idx < depth:
        return
    eng.wait_ge(sem, (idx - depth + 1) * per)


def settle(eng):
    eng.nop(nofuse=True)


def hold(eng, sem, value):
    eng.wait_ge(sem, value)
    settle(eng)


def bc(ap, axis, n):
    v = ap.unsqueeze(axis)
    shape = list(v.shape)
    shape[axis] = n
    return v.broadcast_to(shape)


class Tools:

    def __init__(self, nc, ctx, tag):
        self.nc, self.ctx, self.tag = nc, ctx, tag

    def sb(self, name, shape, dt=F32):
        return self.ctx.enter_context(self.nc.sbuf_tensor(f"{self.tag}_{name}", shape, dt))

    def ps(self, name, shape, dt=F32):
        return self.ctx.enter_context(self.nc.psum_tensor(f"{self.tag}_{name}", shape, dt))

    def sem(self, name):
        return self.ctx.enter_context(self.nc.semaphore(f"{self.tag}_{name}"))


class Chain:

    def __init__(self, eng, sem, base=0):
        self.eng, self.sem, self.base, self.k = eng, sem, base, 0

    def link(self, ins):
        self.k += 1
        ins.then_inc(self.sem, 1)
        return self.k

    def wait(self):
        hold(self.eng, self.sem, self.base + self.k)


def setup(nc, w, io):
    with ExitStack() as ctx:
        t = Tools(nc, ctx, "set")
        wraw = {"q": w["Wq"], "k": w["Wk"], "v": t.sb("raw_v", [P, HM])}
        wT = {n: t.sb(f"T_{n}", [P, PAIRS, P]) for n in "qkv"}
        wo = t.sb("wo", [P, PAIRS, P])
        proj = t.sb("proj", [P, P])
        projT = t.sb("projT", [P, P])
        crow = t.sb("crow", [BATCH, D])
        cT = t.sb("cT", [P, BATCH])
        cs = t.sb("cs", [P, 4, BATCH])
        wmod = t.sb("wmod", [P, 6 * D])
        ln2 = t.sb("ln2", [P, 2])
        gt = t.sb("gt", [P, 2, 4, BATCH])
        pa = [t.ps(f"pa{i}", [P, 4, P]) for i in range(2)]
        pc = t.ps("pc", [P, 512])
        pm = t.ps("pm", [P, 512])
        ident = w["ident"]
        loaded_x, loaded_w, loaded_late = t.sem("loaded_x"), t.sem("loaded_w"), t.sem("loaded_late")
        loaded_c = t.sem("loaded_c")
        cleared, made, drawn = t.sem("cleared"), t.sem("made"), t.sem("drawn")
        turned, turned_used = t.sem("turned"), t.sem("turned_used")
        c_turned, c_done, mod_done, act_e = t.sem("c_turned"), t.sem("c_done"), t.sem("mod_done"), t.sem("act_e")
        vec = t.sem("vec")
        block = ctx.enter_context(nc.Block())

        @block.sync
        def _(sp):
            for n in "qkv":
                sp.dma_start(wraw[n][:], io[f"W{n}"].rearrange("d h k -> d (h k)")).then_inc(loaded_w, 16)
            sp.dma_start(wo[:], io["Wo"].rearrange("(p a) k o -> (a k) p o", a=2)).then_inc(loaded_w, 16)
            sp.wait_ge(cleared, 1)
            for a in range(2):
                sp.dma_start(proj[a * M:(a + 1) * M, a * DH:(a + 1) * DH], io["proj"]).then_inc(loaded_w, 16)
            x = io["x"].rearrange("b (j p) d -> p (b j) d", p=P)
            for g in range(4):
                n = TILES // 4
                sp.dma_start(w["x"][:, g * n:(g + 1) * n, :], x[:, g * n:(g + 1) * n, :]).then_inc(loaded_x, 16)
            for s, v in ((loaded_x, 64), (loaded_w, 96)):
                sp.wait_ge(s, v)

        @block.scalar
        def _(act):
            act.dma_start(crow[:], io["c"]).then_inc(loaded_c, 16)
            act.dma_start(wmod[:], io["wmod"]).then_inc(loaded_c, 16)
            act.dma_start(ln2[:, 0:1], io["ln2_g"].rearrange("(d a) -> d a", a=1)).then_inc(loaded_c, 16)
            act.dma_start(ln2[:, 1:2], io["ln2_b"].rearrange("(d a) -> d a", a=1)).then_inc(loaded_c, 16)
            late = [
                (w["w1"][:], io["W1"]),
                (w["w2"][:], io["W2"].rearrange("(c f) d -> f c d", f=P)),
                (w["b1"][:], io["b1"].rearrange("(c f) -> f c", f=P)),
                (w["b2"][:], io["b2"].rearrange("(a d) -> a d", a=1)),
                (w["ln1"][:, 0:1], io["ln1_g"].rearrange("(d a) -> d a", a=1)),
                (w["ln1"][:, 1:2], io["ln1_b"].rearrange("(d a) -> d a", a=1)),
            ]
            for dst, src in late:
                act.dma_start(dst, src, allow_slow_non_contiguous=True).then_inc(loaded_late, 16)
            act.wait_ge(c_turned, 1)
            nc.scalar.activation(cs[:, 0, :], cT[:], ACT.Exp, scale=-1.0).then_inc(act_e, 1)
            act.wait_ge(loaded_late, 16 * len(late))

        @block.gpsimd
        def _(pool):
            nc.gpsimd.memset(proj[:], 0.0).then_inc(cleared, 1)
            nc.gpsimd.memset(ident[:], 0.0).then_inc(made, 1)
            nc.gpsimd.memset(w["ident16"][:], 0.0).then_inc(made, 1)
            nc.gpsimd.memset(w["ones"][:], 1.0).then_inc(made, 1)
            nc.gpsimd.memset(w["mhalf"][:], -0.5).then_inc(made, 1)
            nc.gpsimd.memset(w["epsk"][:], EPS_KERN).then_inc(made, 1)
            pool.wait_ge(made, 5)
            for m in (ident, w["ident16"]):
                nc.gpsimd.affine_select(out=m[:], in_=m[:], compare_op=ALU.not_equal, fill=1.0, base=0,
                                        pattern=[[-1, P]], channel_multiplier=1).then_inc(drawn, 1)

        groups = [(n, g) for n in "qkv" for g in range(2)]

        @block.tensor
        def _(pe):
            pe.wait_ge(drawn, 2)
            pe.wait_ge(loaded_c, 64)
            nc.tensor.transpose(pc[:, 0:BATCH], crow[:], ident[0:BATCH, 0:BATCH]).then_inc(turned, 1)
            pe.wait_ge(loaded_w, 96)
            nc.tensor.transpose(pm[:, 0:P], proj[:], ident[:]).then_inc(turned, 1)
            for k, (n, g) in enumerate(groups):
                if k >= 2:
                    pe.wait_ge(turned_used, k - 1)
                for q in range(4):
                    p = 4 * g + q
                    last = nc.tensor.transpose(pa[k % 2][:, q, :], wraw[n][:, p * P:(p + 1) * P], ident[:])
                last.then_inc(turned, 1)
            pe.wait_ge(c_done, 1)
            for s in range(6):
                last = nc.tensor.matmul(pm[:, s * BATCH:(s + 1) * BATCH], wmod[:, s * D:(s + 1) * D],
                                        cs[:, 3, :], start=True, stop=True)
            last.then_inc(mod_done, 1)
            k = len(groups)
            pe.wait_ge(turned_used, k)
            for n in "qk":
                for g in range(2):
                    pe.wait_ge(turned_used, k - 1)
                    for q in range(4):
                        last = nc.tensor.matmul(pa[k % 2][:, q, :], wT[n][:, 4 * g + q, :], projT[:], start=True, stop=True)
                    last.then_inc(turned, 1)
                    k += 1
            for g in range(4):
                pe.wait_ge(turned_used, k - 1)
                for q in range(4):
                    p = 4 * (g // 2) + q
                    r = slice((g % 2) * DH, (g % 2 + 1) * DH)
                    last = nc.tensor.matmul(pa[k % 2][:, q, :], wT["v"][r, p, :], wo[r, p, :], start=True, stop=True)
                last.then_inc(turned, 1)
                k += 1

        @block.vector
        def _(dve):
            c = Chain(dve, vec)
            dve.wait_ge(turned, 1)
            nc.vector.tensor_copy(cT[:], pc[:, 0:BATCH]).then_inc(c_turned, 1)
            dve.wait_ge(turned, 2)
            c.link(nc.vector.tensor_scalar(projT[:], pm[:, 0:P], DN, None, MUL))
            dve.wait_ge(act_e, 1)
            c.link(nc.vector.tensor_scalar(cs[:, 1, :], cs[:, 0, :], 1.0, None, ADD))
            c.wait()
            c.link(nc.vector.reciprocal(cs[:, 2, :], cs[:, 1, :]))
            c.wait()
            nc.vector.tensor_tensor(cs[:, 3, :], cs[:, 2, :], cT[:], MUL).then_inc(c_done, 1)
            k = 2
            for n, g in groups:
                dve.wait_ge(turned, k + 1)
                nc.vector.tensor_copy(wT[n][:, 4 * g:4 * g + 4, :], pa[k % 2][:]).then_inc(turned_used, 1)
                k += 1
            dst = [w["WqP"][:, g * 512:(g + 1) * 512] for g in range(2)] + [w["WkP"][:, g * 512:(g + 1) * 512] for g in range(2)]
            wvo = w["Wvo"][:].rearrange("p (r a o) -> p a r o", a=2, o=D)
            dst = [d.rearrange("p (q o) -> p q o", q=4) for d in dst]
            dst += [wvo[:, g % 2, 4 * (g // 2):4 * (g // 2) + 4, :] for g in range(4)]
            for d in dst:
                dve.wait_ge(turned, k + 1)
                nc.vector.tensor_copy(d, pa[k % 2][:]).then_inc(turned_used, 1)
                k += 1
            dve.wait_ge(mod_done, 1)
            dve.wait_ge(loaded_c, 64)
            mod = w["mod"]
            pmv = pm[:, 0:6 * BATCH].rearrange("p (s b) -> p s b", s=6)
            for col, s in ((SA, 0), (SB, 3)):
                nc.vector.tensor_copy(mod[:, :, col], pmv[:, s, :])
            for col, s in ((CA1, 1), (CB1, 4)):
                nc.vector.tensor_scalar(mod[:, :, col], pmv[:, s, :], 1.0, None, ADD)
            for k, s in ((0, 2), (1, 5)):
                c.link(nc.vector.tensor_copy(gt[:, k, 0, :], pmv[:, s, :]))
            c.wait()
            for k in range(2):
                c.link(nc.vector.scalar_tensor_tensor(gt[:, k, 1, :], gt[:, k, 0, :], -1.0, gt[:, k, 0, :], MUL, MAX))
                c.link(nc.vector.tensor_scalar(gt[:, k, 2, :], gt[:, k, 0, :], 0.0, 2.0, ALU.is_ge, MUL))
            c.wait()
            for k in range(2):
                c.link(nc.vector.tensor_scalar(gt[:, k, 3, :], gt[:, k, 1, :], 0.25, None, MAX))
            c.wait()
            for k in range(2):
                c.link(nc.vector.scalar_tensor_tensor(gt[:, k, 0, :], gt[:, k, 2, :], -1.0, gt[:, k, 3, :], ADD, MUL))
            c.wait()
            nc.vector.tensor_scalar(mod[:, :, GAG], gt[:, 0, 0, :], ln2[:, 0:1], None, MUL)
            nc.vector.tensor_scalar(mod[:, :, GAB], gt[:, 0, 0, :], ln2[:, 1:2], None, MUL)
            nc.vector.tensor_scalar(mod[:, :, GB], gt[:, 1, 0, :], 1.0 / WSCALE, None, MUL)


def keys_phase(nc, w, io):
    with ExitStack() as ctx:
        t = Tools(nc, ctx, "key")
        st6 = t.sb("st6", [P, 2, JT, 6])
        mv = t.sb("mv", [P, 2, JT, 2])
        rs = t.sb("rs", [P, 2, JT])
        ve = t.sb("ve", [P, 2, JT])
        xn = t.sb("xn", [P, 2, JT, D])
        hT = t.sb("hT", [P, 2, SEQ])
        h = t.sb("h", [P, 2, JT, D])
        sq = t.sb("sq", [P, 2, 512])
        diag = t.sb("diag", [P, 2, HEADS // 2])
        arg = t.sb("arg", [P, 2, JT, HM])
        rmax = t.sb("rmax", [P, 2, 2 * JT])
        bmax = t.sb("bmax", [P, 2, 1])
        cmax = t.sb("cmax", [P, 2, 1])
        ncmax = t.sb("ncmax", [P, 2, 1])
        pT = t.ps("pT", [P, 2, SEQ])
        pM = t.ps("pM", [P, 512])
        pK = [t.ps(f"pK{u}", [P, 512]) for u in range(2)]
        pD = [t.ps(f"pD{u}", [P, 512]) for u in range(2)]
        pG = [t.ps(f"pG{u}", [P, 512]) for u in range(2)]
        stats, var_e, rstd = t.sem("stats"), t.sem("var_e"), t.sem("rstd")
        agg = t.sem("agg")
        xn_ready, xT_ready, hT_ready, h_back, h_ready = (t.sem(n) for n in ("xn_ready", "xT_ready", "hT_ready", "h_back", "h_ready"))
        hT_saved, hsum_done = t.sem("hT_saved"), t.sem("hsum_done")
        k_ready, k_squared, sq_summed = t.sem("k_ready"), t.sem("k_squared"), t.sem("sq_summed")
        dash_ready, dash_max, arg_ready = t.sem("dash_ready"), t.sem("dash_max"), t.sem("arg_ready")
        bmax_ready, cmax_ready, ncmax_ready, cmax_kept = (t.sem(n) for n in ("bmax_ready", "cmax_ready", "ncmax_ready", "cmax_kept"))
        kf_ready, g_ready, g_kept, ks_ready, ks_kept = (t.sem(n) for n in ("kf_ready", "g_ready", "g_kept", "ks_ready", "ks_kept"))
        block = ctx.enter_context(nc.Block())
        x, mod, ident = w["x"], w["mod"], w["ident"]

        @block.vector
        def _(dve):
            def body(it, par, pair):
                b, q = it - 1, 1 - par
                if inside(b, BATCH):
                    dve.wait_ge(rstd, b + 1)
                    wait_free(dve, xT_ready, b)
                    for j in range(JT):
                        nc.vector.tensor_scalar(xn[:, q, j, :], x[:, b * JT + j, :], mv[:, q, j, 0:1], rs[:, q, j:j + 1],
                                                SUB, MUL).then_inc(xn_ready, 1)
                b = it
                if inside(b, BATCH):
                    wait_free(dve, rstd, b)
                    wait_free(dve, xn_ready, b, per=JT)
                    settle(dve)
                    for j in range(JT):
                        nc.vector.bn_stats(st6[:, par, j, :], x[:, b * JT + j, :]).then_inc(stats, 1)
                    hold(dve, stats, (b + 1) * JT)
                    for j in range(JT):
                        nc.vector.bn_aggr(mv[:, par, j, :], st6[:, par, j, :]).then_inc(agg, 1)
                b = it - 2
                if inside(b, BATCH):
                    for j in range(JT):
                        for u in range(2):
                            n = (b * JT + j) * 2 + u
                            dve.wait_ge(k_squared, n + 1)
                            wait_free(dve, arg_ready, n)
                            nc.vector.tensor_reduce(diag[:, u, :], sq[:, u, :].rearrange("p (h k) -> p h k", k=DH),
                                                    AX.X, ADD).then_inc(sq_summed, 1)
                            dve.wait_ge(dash_ready, n + 1)
                            if j == 0 and u == 0:
                                wait_free(dve, bmax_ready, b)
                            nc.vector.tensor_reduce(rmax[:, par, 2 * j + u:2 * j + u + 1], pD[u][:], AX.X, MAX).then_inc(dash_max, 1)
                            dve.wait_ge(sq_summed, n + 1)
                            if j == 0 and u == 0:
                                wait_free(dve, ks_ready, b)
                            nc.vector.tensor_tensor(
                                arg[:, par, j, u * 512:(u + 1) * 512].rearrange("p (h m) -> p h m", m=M),
                                pD[u][:].rearrange("p (h m) -> p h m", m=M), bc(diag[:, u, :], 2, M), SUB).then_inc(arg_ready, 1)
                    dve.wait_ge(dash_max, (b + 1) * 2 * JT)
                    wait_free(dve, cmax_ready, b)
                    nc.vector.tensor_reduce(bmax[:, par, :], rmax[:, par, :], AX.X, MAX).then_inc(bmax_ready, 1)
                b, q = it - 1, 1 - par
                if inside(b, BATCH):
                    dve.wait_ge(hT_ready, b + 1)
                    nc.vector.tensor_reduce(w["hsum"][:, bass.ds(b, 1)], hT[:, q, :], AX.X, ADD).then_inc(hsum_done, 1)
                b = it - 2
                if inside(b, BATCH):
                    dve.wait_ge(cmax_ready, b + 1)
                    wait_free(dve, kf_ready, b, per=JT)
                    nc.vector.tensor_scalar(ncmax[:, par, :], cmax[:, par, :], -1.0, None, MUL).then_inc(ncmax_ready, 1)
                    nc.vector.tensor_copy(w["cmax"][:, bass.ds(b, 1)], cmax[:, par, :]).then_inc(cmax_kept, 1)

            sweep(dve, BATCH, 2, body)

        @block.gpsimd
        def _(pool):
            def body(it, par, pair):
                b = it
                if inside(b, BATCH):
                    pool.wait_ge(agg, (b + 1) * JT)
                    wait_free(pool, xn_ready, b, per=JT)
                    settle(pool)
                    nc.gpsimd.tensor_scalar(ve[:, par, :], mv[:, par, :, 1], EPS_LN, None, ADD).then_inc(var_e, 1)
                    pool.wait_ge(var_e, b + 1)
                    nc.gpsimd.tensor_tensor(rs[:, par, :], ve[:, par, :], w["mhalf"][:, 0:JT], ALU.pow).then_inc(rstd, 1)
                b = it - 2
                if inside(b, BATCH):
                    pool.wait_ge(bmax_ready, b + 1)
                    wait_free(pool, ncmax_ready, b)
                    wait_free(pool, cmax_kept, b)
                    settle(pool)
                    nc.gpsimd.partition_all_reduce(cmax[:, par, :], bmax[:, par, :], P, bass.bass_isa.ReduceOp.max).then_inc(cmax_ready, 1)

            sweep(pool, BATCH, 2, body)

        @block.tensor
        def _(pe):
            def project(b, par, j):
                tok = hT[:, par, j * P:(j + 1) * P]
                for u in range(2):
                    n = (b * JT + j) * 2 + u
                    wait_free(pe, k_squared, n)
                    nc.tensor.matmul(pK[u][:], tok, w["Wk"][:, u * 512:(u + 1) * 512], start=True, stop=True).then_inc(k_ready, 1)
                    wait_free(pe, arg_ready, n)
                    nc.tensor.matmul(pD[u][:], tok, w["WkP"][:, u * 512:(u + 1) * 512], start=True, stop=True).then_inc(dash_ready, 1)

            def body(it, par, pair):
                b, q = it - 1, 1 - par
                for j in range(JT):
                    if inside(it - 2, BATCH):
                        project(it - 2, par, j)
                    if j == 0 and inside(b, BATCH):
                        wait_free(pe, h_ready, b, depth=1)
                        for i in range(JT):
                            pe.wait_ge(xn_ready, b * JT + i + 1)
                            last = nc.tensor.transpose(pT[:, 0, i * P:(i + 1) * P], xn[:, q, i, :], ident[:])
                        last.then_inc(xT_ready, 1)
                b, q = it - 3, 1 - par
                if inside(b, BATCH):
                    pe.wait_ge(kf_ready, (b + 1) * JT)
                    for u in range(2):
                        wait_free(pe, g_kept, b * 2 + u)
                        for j in range(JT):
                            last = nc.tensor.matmul(pG[u][:], h[:, q, j, :], arg[:, q, j, u * 512:(u + 1) * 512],
                                                    start=(j == 0), stop=(j == JT - 1))
                        last.then_inc(g_ready, 1)
                    wait_free(pe, ks_kept, b, depth=1)
                    for p in range(PAIRS):
                        for j in range(JT):
                            last = nc.tensor.matmul(pM[:, p:p + 1], arg[:, q, j, p * P:(p + 1) * P], w["ones"][:, 0:1],
                                                    start=(j == 0), stop=(j == JT - 1))
                    last.then_inc(ks_ready, 1)
                b, q = it - 1, 1 - par
                if inside(b, BATCH):
                    pe.wait_ge(hT_ready, b + 1)
                    for j in range(JT):
                        last = nc.tensor.transpose(pT[:, 1, j * P:(j + 1) * P], hT[:, q, j * P:(j + 1) * P], ident[:])
                    last.then_inc(h_back, 1)

            sweep(pe, BATCH, 3, body)

        @block.scalar
        def _(act):
            def body(it, par, pair):
                b, q = it - 3, 1 - par
                if inside(b, BATCH):
                    act.wait_ge(ncmax_ready, b + 1)
                    act.wait_ge(arg_ready, (b + 1) * 2 * JT)
                    for j in range(JT):
                        nc.scalar.activation(arg[:, q, j, :], arg[:, q, j, :], ACT.Exp, bias=ncmax[:, q, :]).then_inc(kf_ready, 1)
                for j in range(JT):
                    b = it - 2
                    if inside(b, BATCH):
                        for u in range(2):
                            n = (b * JT + j) * 2 + u
                            act.wait_ge(k_ready, n + 1)
                            wait_free(act, sq_summed, n)
                            nc.scalar.activation(sq[:, u, :], pK[u][:], ACT.Square, scale=DN * 0.5 ** 0.5).then_inc(k_squared, 1)
                    b, q = it - 1, 1 - par
                    if j == 0 and inside(b, BATCH):
                        act.wait_ge(xT_ready, b + 1)
                        wait_free(act, dash_ready, b, per=2 * JT)
                        wait_free(act, h_back, b)
                        wait_free(act, hT_saved, b, per=16)
                        wait_free(act, hsum_done, b)
                        nc.scalar.activation(hT[:, q, :], pT[:, 0, :], ACT.Identity, bias=mod[:, b, SA:SA + 1],
                                             scale=mod[:, b, CA1:CA1 + 1]).then_inc(hT_ready, 1)
                b = it - 3
                if inside(b, BATCH):
                    for u in range(2):
                        act.wait_ge(g_ready, b * 2 + u + 1)
                        nc.scalar.activation(w["G"][:, b, u * 512:(u + 1) * 512], pG[u][:], ACT.Copy).then_inc(g_kept, 1)
                    act.wait_ge(ks_ready, b + 1)
                    nc.scalar.activation(w["ksum"][:, b, :], pM[:, 0:PAIRS], ACT.Copy).then_inc(ks_kept, 1)
                b, q = it - 1, 1 - par
                if inside(b, BATCH):
                    act.wait_ge(h_back, b + 1)
                    wait_free(act, g_ready, b, per=2)
                    nc.scalar.activation(h[:, q, :, :], pT[:, 1, :].rearrange("p (j d) -> p j d", j=JT), ACT.Copy).then_inc(h_ready, 1)

            sweep(act, BATCH, 3, body)

        @block.sync
        def _(sp):
            def body(it, par, pair):
                b = it
                if inside(b, BATCH):
                    hold(sp, hT_ready, b + 1)
                    wait_free(sp, hT_saved, b, per=16, depth=1)
                    settle(sp)
                    sp.dma_start(w["hT"][:, b, :], hT[:, par, :]).then_inc(hT_saved, 16)

            sweep(sp, BATCH, 0, body)
            sp.wait_ge(hT_saved, 16 * BATCH)


def queries_phase(nc, w):
    with ExitStack() as ctx:
        t = Tools(nc, ctx, "qry")
        gmax = t.sb("gmax", [P, 2])
        sc = t.sb("sc", [P, BATCH])
        ks = t.sb("ks", [P, BATCH, PAIRS])
        ksd = t.sb("ksd", [P, BATCH, PAIRS, 2])
        ehs = t.sb("ehs", [P, BATCH])
        gs = t.sb("gs", [P, HM])
        kv = t.sb("kv", [P, PAIRS, D])
        hTq = t.sb("hTq", [P, 2, P])
        hTr = t.sb("hTr", [P, 2, P])
        sq = t.sb("sq", [P, 2, 512])
        diag = t.sb("diag", [P, 2, HEADS // 2])
        hmax = t.sb("hmax", [P, 2, HEADS // 2])
        off = t.sb("off", [P, 2, HEADS // 2])
        qf = t.sb("qf", [P, 2, HM])
        qfT = t.sb("qfT", [P, PAIRS, P])
        rden = t.sb("rden", [P, HEADS])
        qn = t.sb("qn", [P, 2, HM])
        qnT = t.sb("qnT", [P, PAIRS, P])
        pK = [t.ps(f"pK{u}", [P, 512]) for u in range(2)]
        pD = [t.ps(f"pD{u}", [P, 512]) for u in range(2)]
        pE = [t.ps(f"pE{u}", [P, 4, P]) for u in range(2)]
        pS = t.ps("pS", [P, 512])
        pO = t.ps("pO", [P, 512])
        pre, pre_a = t.sem("pre"), t.sem("pre_a")
        hq_loaded = [t.sem(f"hq_loaded{i}") for i in range(2)]
        hr_loaded = [t.sem(f"hr_loaded{i}") for i in range(2)]
        (q_ready, q_squared, sq_summed, dash_ready, dash_max, off_ready, arg_ready, exp_ready) = (
            t.sem(n) for n in ("q_ready", "q_squared", "sq_summed", "dash_ready", "dash_max", "off_ready", "arg_ready", "exp_ready"))
        (qf_turned, qf_kept, den_ready, rden_ready, qn_ready, qn_turned, qn_kept) = (
            t.sem(n) for n in ("qf_turned", "qf_kept", "den_ready", "rden_ready", "qn_ready", "qn_turned", "qn_kept"))
        (gs_ready, kv_ready, kv_kept, out_ready, out_kept) = (
            t.sem(n) for n in ("gs_ready", "kv_ready", "kv_kept", "out_ready", "out_kept"))
        block = ctx.enter_context(nc.Block())
        ident = w["ident"]

        @block.sync
        def _(sp):
            def body(it, par, pair):
                if inside(it, TILES):
                    wait_free(sp, dash_ready, it, per=2)
                    sp.dma_start(hTq[:, par, :], w["hT"][:, pair, par * P:(par + 1) * P]).then_inc(hq_loaded[par], 16)
                    wait_free(sp, out_ready, it)
                    sp.dma_start(hTr[:, par, :], w["hT"][:, pair, par * P:(par + 1) * P]).then_inc(hr_loaded[par], 16)

            sweep(sp, TILES, 0, body)

        @block.vector
        def _(dve):
            c = Chain(dve, pre)
            c.link(nc.vector.tensor_reduce(gmax[:, 0:1], w["cmax"][:], AX.X, MAX))
            c.link(nc.vector.memset(ksd[:], 0.0))
            nc.vector.tensor_scalar(ehs[:], w["hsum"][:], EPS_KERN, None, MUL)
            c.wait()
            c.link(nc.vector.tensor_scalar(gmax[:, 1:2], gmax[:, 0:1], -1.0, None, MUL))
            dve.wait_ge(pre_a, 1)
            c.link(nc.vector.tensor_tensor(ks[:], w["ksum"][:], bc(sc[:], 2, PAIRS), MUL))
            c.wait()
            for a in range(2):
                r = slice(a * M, (a + 1) * M)
                c.link(nc.vector.tensor_scalar(ksd[r, :, :, a], ks[r, :, :], SEQ * EPS_KERN, None, ADD))

            def features(n, u):
                k = n * 2 + u
                heads = qf_v[:, u * 8:(u + 1) * 8, :]
                dve.wait_ge(dash_ready, k + 1)
                wait_free(dve, off_ready, k)
                nc.vector.tensor_reduce(hmax[:, u, :], pD[u][:].rearrange("p (h m) -> p h m", m=M), AX.X, MAX).then_inc(dash_max, 1)
                dve.wait_ge(q_squared, k + 1)
                wait_free(dve, off_ready, k)
                nc.vector.tensor_reduce(diag[:, u, :], sq[:, u, :].rearrange("p (h k) -> p h k", k=DH), AX.X, ADD).then_inc(sq_summed, 1)
                dve.wait_ge(sq_summed, k + 1)
                dve.wait_ge(dash_max, k + 1)
                wait_free(dve, arg_ready, k)
                nc.vector.tensor_tensor(off[:, u, :], hmax[:, u, :], diag[:, u, :], ADD).then_inc(off_ready, 1)
                dve.wait_ge(off_ready, k + 1)
                wait_free(dve, qf_turned, n, per=2)
                wait_free(dve, qn_ready, n)
                nc.vector.tensor_tensor(heads, pD[u][:].rearrange("p (h m) -> p h m", m=M), bc(off[:, u, :], 2, M), SUB).then_inc(arg_ready, 1)

            def body(it, par, pair):
                nonlocal qf_v
                n = it
                qf_v = qf[:, par, :].rearrange("p (h m) -> p h m", m=M)
                if inside(n, TILES):
                    features(n, 0)
                n, q = it - 1, 1 - par
                if inside(n, TILES):
                    dve.wait_ge(den_ready, n + 1)
                    wait_free(dve, qn_ready, n, depth=1)
                    nc.vector.reciprocal(rden[:], pS[:, 0:HEADS]).then_inc(rden_ready, 1)
                    dve.wait_ge(rden_ready, n + 1)
                    wait_free(dve, qn_turned, n, per=2)
                    nc.vector.scalar_tensor_tensor(qn[:, q, :].rearrange("p (h m) -> p h m", m=M),
                                                   qf[:, q, :].rearrange("p (h m) -> p h m", m=M), EPS_KERN,
                                                   bc(rden[:], 2, M), ADD, MUL).then_inc(qn_ready, 1)
                if par == 1 and inside(pair, BATCH):
                    wait_free(dve, kv_ready, pair, per=2, depth=1)
                    nc.vector.tensor_scalar(gs[:], w["G"][:, pair, :], sc[:, bass.ds(pair, 1)], ehs[:, bass.ds(pair, 1)],
                                            MUL, ADD).then_inc(gs_ready, 1)
                if inside(it, TILES):
                    features(it, 1)

            qf_v = None
            sweep(dve, TILES, 1, body)

        @block.scalar
        def _(act):
            act.wait_ge(pre, 3)
            nc.scalar.activation(sc[:], w["cmax"][:], ACT.Exp, bias=gmax[:, 1:2]).then_inc(pre_a, 1)

            def square(n, u):
                k = n * 2 + u
                act.wait_ge(q_ready, k + 1)
                wait_free(act, sq_summed, k)
                nc.scalar.activation(sq[:, u, :], pK[u][:], ACT.Square, scale=DN * 0.5 ** 0.5).then_inc(q_squared, 1)

            def body(it, par, pair):
                n = it - 2
                if inside(n, TILES):
                    for u in range(2):
                        act.wait_ge(qn_turned, n * 2 + u + 1)
                        wait_free(act, out_ready, n, depth=1)
                        nc.scalar.activation(qnT[:, 4 * u:4 * u + 4, :], pE[u][:], ACT.Copy).then_inc(qn_kept, 1)
                if inside(it, TILES):
                    square(it, 0)
                n = it - 1
                if inside(n, TILES):
                    for u in range(2):
                        act.wait_ge(qf_turned, n * 2 + u + 1)
                        wait_free(act, den_ready, n, depth=1)
                        nc.scalar.activation(qfT[:, 4 * u:4 * u + 4, :], pE[u][:], ACT.Identity, bias=w["epsk"][:]).then_inc(qf_kept, 1)
                n = it
                if inside(n, TILES):
                    act.wait_ge(arg_ready, n * 2 + 1)
                    nc.scalar.activation(qf[:, par, 0:512], qf[:, par, 0:512], ACT.Exp).then_inc(exp_ready, 1)
                n = it - 2
                if inside(n, TILES):
                    act.wait_ge(out_ready, n + 1)
                    nc.scalar.activation(w["x1"][:, n, :], pO[:, 0:D], ACT.Copy).then_inc(out_kept, 1)
                n = it
                if inside(n, TILES):
                    square(n, 1)
                    act.wait_ge(arg_ready, n * 2 + 2)
                    nc.scalar.activation(qf[:, par, 512:1024], qf[:, par, 512:1024], ACT.Exp).then_inc(exp_ready, 1)
                if par == 1 and inside(pair, BATCH):
                    for u in range(2):
                        act.wait_ge(kv_ready, pair * 2 + u + 1)
                        wait_free(act, out_ready, pair, per=2, depth=1)
                        nc.scalar.activation(kv[:, 4 * u:4 * u + 4, :], pE[u][:], ACT.Copy).then_inc(kv_kept, 1)

            sweep(act, TILES, 2, body)

        @block.tensor
        def _(pe):
            pe.wait_ge(pre, 6)

            def project(n, par, pair, u):
                k = n * 2 + u
                if u == 0:
                    pe.wait_ge(hq_loaded[par], pair * 16 + 16)
                wait_free(pe, q_squared, k)
                nc.tensor.matmul(pK[u][:], hTq[:, par, :], w["Wq"][:, u * 512:(u + 1) * 512], start=True, stop=True).then_inc(q_ready, 1)
                wait_free(pe, arg_ready, k)
                nc.tensor.matmul(pD[u][:], hTq[:, par, :], w["WqP"][:, u * 512:(u + 1) * 512], start=True, stop=True).then_inc(dash_ready, 1)

            def body(it, par, pair):
                n = it - 2
                if inside(n, TILES):
                    pe.wait_ge(qn_ready, n + 1)
                    for u in range(2):
                        if par == 0:
                            pe.wait_ge(kv_kept, (pair - 1) * 2 + u + 1)
                        elif inside(it - 2, TILES):
                            pe.wait_ge(qf_kept, n * 2 + u + 1)
                        for q in range(4):
                            p = 4 * u + q
                            last = nc.tensor.transpose(pE[u][:, q, :], qn[:, par, p * P:(p + 1) * P], ident[:])
                        last.then_inc(qn_turned, 1)
                if inside(it, TILES):
                    project(it, par, pair, 0)
                n = it - 1
                if inside(n, TILES):
                    for u in range(2):
                        pe.wait_ge(exp_ready, n * 2 + u + 1)
                        if inside(it - 2, TILES):
                            pe.wait_ge(qn_kept, (it - 2) * 2 + u + 1)
                        for q in range(4):
                            p = 4 * u + q
                            last = nc.tensor.transpose(pE[u][:, q, :], qf[:, 1 - par, p * P:(p + 1) * P], ident[:])
                        last.then_inc(qf_turned, 1)
                n = it - 2
                if inside(n, TILES):
                    pe.wait_ge(qn_kept, n * 2 + 2)
                    pe.wait_ge(hr_loaded[par], pair * 16)
                    pe.wait_ge(kv_kept, (pair - 1) * 2 + 2)
                    wait_free(pe, out_kept, n, depth=1)
                    for p in range(PAIRS):
                        nc.tensor.matmul(pO[:, 0:D], qnT[:, p, :], kv[:, p, :], start=(p == 0), stop=False)
                    nc.tensor.matmul(pO[:, 0:D], hTr[:, par, :], ident[:], start=False, stop=True).then_inc(out_ready, 1)
                n = it - 1
                if inside(n, TILES):
                    b = pair if par == 1 else pair - 1
                    pe.wait_ge(qf_kept, n * 2 + 2)
                    wait_free(pe, rden_ready, n, depth=1)
                    for p in range(PAIRS):
                        last = nc.tensor.matmul(pS[:, 2 * p:2 * p + 2], qfT[:, p, :], ksd[:, b, p, :], start=True, stop=True)
                    last.then_inc(den_ready, 1)
                if inside(it, TILES):
                    project(it, par, pair, 1)
                if par == 1 and inside(pair, BATCH):
                    pe.wait_ge(gs_ready, pair + 1)
                    for u in range(2):
                        pe.wait_ge(qf_kept, (it - 1) * 2 + u + 1)
                        for q in range(4):
                            for a in range(2):
                                h = 2 * (4 * u + q) + a
                                last = nc.tensor.matmul(pE[u][a * M:(a + 1) * M, q, :], gs[:, h * M:(h + 1) * M],
                                                        w["Wvo"][:, h * D:(h + 1) * D], start=True, stop=True)
                        last.then_inc(kv_ready, 1)

            sweep(pe, TILES, 2, body)


def ffn_phase(nc, w, io):
    with ExitStack() as ctx:
        t = Tools(nc, ctx, "ffn")
        st6 = [t.sb(f"st6{i}", [P, JT, 6]) for i in range(3)]
        mv = [t.sb(f"mv{i}", [P, 2, JT, 2]) for i in range(3)]
        ve = [t.sb(f"ve{i}", [P, JT]) for i in range(3)]
        rs = [t.sb(f"rs{i}", [P, 2, JT]) for i in range(3)]
        xn = [t.sb(f"xn{i}", [P, JT, D]) for i in range(3)]
        o1T = t.sb("o1T", [P, 2, SEQ])
        z = t.sb("z", [P, FC, SEQ])
        ez = t.sb("ez", [P, FC, SEQ])
        hid = t.sb("hid", [P, FC, SEQ])
        yT = t.sb("yT", [P, SEQ])
        h2T = t.sb("h2T", [P, 2, SEQ])
        h2 = t.sb("h2", [P, 2, JT, D + 1])
        pF = t.ps("pF", [P, FC, SEQ])
        pA = t.ps("pA", [P, 512])
        pA2 = t.ps("pA2", [P, 512])
        pX = t.ps("pX", [P, JT, D])
        pXf = t.ps("pXf", [P, JT, D])
        pB = t.ps("pB", [P, JT, D])
        pC = t.ps("pC", [P, D + 1])
        stats = [t.sem(f"stats{i}") for i in range(3)]
        agg = [t.sem(f"agg{i}") for i in range(3)]
        vard = [t.sem(f"vard{i}") for i in range(3)]
        rstd = [t.sem(f"rstd{i}") for i in range(3)]
        xn_ready = [t.sem(f"xn_ready{i}") for i in range(3)]
        turned = [t.sem(f"turned{i}") for i in range(3)]
        o1_ready, y_ready, h2T_ready = t.sem("o1_ready"), t.sem("y_ready"), t.sem("h2T_ready")
        f1_ready, z_ready, min_ready, e_ready, hid_ready = (t.sem(n) for n in ("f1_ready", "z_ready", "min_ready", "e_ready", "hid_ready"))
        x2_ready, y_back, xm_ready, h2_back, h2_ready = (t.sem(n) for n in ("x2_ready", "y_back", "xm_ready", "h2_back", "h2_ready"))
        cov_ready, cov_added, h2T_saved = t.sem("cov_ready"), t.sem("cov_added"), t.sem("h2T_saved")
        init = t.sem("init")
        block = ctx.enter_context(nc.Block())
        ident, mod = w["ident"], w["mod"]
        EPS = (EPS_LN_ATTN, EPS_LN_ATTN, EPS_LN)

        @block.vector
        def _(dve):
            nc.vector.memset(w["cov"][:], 0.0).then_inc(cov_added, 1)
            for k in range(2):
                nc.vector.memset(h2[:, k, :, D:D + 1], 1.0).then_inc(init, 1)

            def statistics(i, b, par, src):
                wait_free(dve, vard[i], b)
                if i != 1:
                    wait_free(dve, xn_ready[i], b)
                settle(dve)
                for j in range(JT):
                    nc.vector.bn_stats(st6[i][:, j, :], src(j)).then_inc(stats[i], 1)
                hold(dve, stats[i], (b + 1) * JT)
                for j in range(JT):
                    nc.vector.bn_aggr(mv[i][:, par, j, :], st6[i][:, j, :]).then_inc(agg[i], 1)

            def normalise(i, b, par, src):
                dve.wait_ge(rstd[i], b + 1)
                wait_free(dve, turned[i], b, depth=1)
                for j in range(JT):
                    last = nc.vector.tensor_scalar(xn[i][:, j, :], src(j), mv[i][:, par, j, 0:1], rs[i][:, par, j:j + 1], SUB, MUL)
                last.then_inc(xn_ready[i], 1)

            def body(it, par, pair):
                q = 1 - par
                b = it - 2
                if inside(b, BATCH):
                    normalise(1, b, par, lambda j: pX[:, j, :])
                b = it - 3
                if inside(b, BATCH):
                    normalise(2, b, q, lambda j: w["x"][:, b * JT + j, :])
                b = it
                if inside(b, BATCH):
                    wait_free(dve, agg[0], b, per=JT, depth=1)
                    statistics(0, b, par, lambda j: w["x1"][:, b * JT + j, :])
                b = it - 1
                if inside(b, BATCH):
                    dve.wait_ge(z_ready, (b + 1) * FC)
                    wait_free(dve, hid_ready, b, depth=1)
                    nc.vector.tensor_scalar(ez[:], z[:], 0.0, None, MIN).then_inc(min_ready, 1)
                b = it - 4
                if inside(b, BATCH):
                    dve.wait_ge(cov_ready, b + 1)
                    dve.wait_ge(cov_added, b + 1)
                    nc.vector.tensor_tensor(w["cov"][:], pC[:], w["cov"][:], ADD).then_inc(cov_added, 1)
                b = it
                if inside(b, BATCH):
                    normalise(0, b, par, lambda j: w["x1"][:, b * JT + j, :])
                b = it - 1
                if inside(b, BATCH):
                    dve.wait_ge(e_ready, b + 1)
                    wait_free(dve, x2_ready, b, depth=1)
                    nc.vector.scalar_tensor_tensor(hid[:], ez[:], -1.0, z[:], ADD, MAX).then_inc(hid_ready, 1)
                b = it - 2
                if inside(b, BATCH):
                    dve.wait_ge(y_back, b + 1)
                    nc.vector.tensor_tensor(w["x"][:, bass.ds(b * JT, JT), :], pB[:], w["x"][:, bass.ds(b * JT, JT), :], ADD).then_inc(xm_ready, 1)
                b = it - 1
                if inside(b, BATCH):
                    dve.wait_ge(x2_ready, b + 1)
                    wait_free(dve, agg[1], b, per=JT, depth=1)
                    statistics(1, b, q, lambda j: pX[:, j, :])
                b = it - 2
                if inside(b, BATCH):
                    dve.wait_ge(xm_ready, b + 1)
                    wait_free(dve, agg[2], b, per=JT, depth=1)
                    statistics(2, b, par, lambda j: w["x"][:, b * JT + j, :])

            sweep(dve, BATCH, 4, body)

        @block.gpsimd
        def _(pool):
            def body(it, par, pair):
                for i in range(3):
                    b, q = it - i, (par - i) % 2
                    if inside(b, BATCH):
                        pool.wait_ge(agg[i], (b + 1) * JT)
                        wait_free(pool, rstd[i], b, depth=1)
                        wait_free(pool, xn_ready[i], b)
                        settle(pool)
                        nc.gpsimd.tensor_scalar(ve[i][:], mv[i][:, q, :, 1], EPS[i], None, ADD).then_inc(vard[i], 1)
                        pool.wait_ge(vard[i], b + 1)
                        nc.gpsimd.tensor_tensor(rs[i][:, q, :], ve[i][:], w["mhalf"][:, 0:JT], ALU.pow).then_inc(rstd[i], 1)

            sweep(pool, BATCH, 2, body)

        @block.scalar
        def _(act):
            def body(it, par, pair):
                q = 1 - par
                b = it - 1
                if inside(b, BATCH):
                    act.wait_ge(f1_ready, b + 1)
                    wait_free(act, hid_ready, b, depth=1)
                    for f in range(FC):
                        nc.scalar.activation(z[:, f, :], pF[:, f, :], ACT.Identity, bias=w["b1"][:, f:f + 1]).then_inc(z_ready, 1)
                b = it - 2
                if inside(b, BATCH):
                    act.wait_ge(turned[1], b + 1)
                    wait_free(act, y_back, b, depth=1)
                    nc.scalar.activation(yT[:], pA2[:, 0:SEQ], ACT.Identity, bias=mod[:, b, GAB:GAB + 1], scale=mod[:, b, GAG:GAG + 1]).then_inc(y_ready, 1)
                b = it - 1
                if inside(b, BATCH):
                    act.wait_ge(min_ready, b + 1)
                    nc.scalar.activation(ez[:], ez[:], ACT.Exp).then_inc(e_ready, 1)
                b = it - 3
                if inside(b, BATCH):
                    act.wait_ge(turned[2], b + 1)
                    wait_free(act, h2_back, b)
                    wait_free(act, h2T_saved, b, per=16)
                    nc.scalar.activation(h2T[:, q, :], pA[:, 0:SEQ], ACT.Identity, bias=mod[:, b, SB:SB + 1], scale=mod[:, b, CB1:CB1 + 1]).then_inc(h2T_ready, 1)
                b = it
                if inside(b, BATCH):
                    act.wait_ge(turned[0], b + 1)
                    wait_free(act, x2_ready, b)
                    nc.scalar.activation(o1T[:, par, :], pA[:, 0:SEQ], ACT.Identity, bias=w["ln1"][:, 1:2], scale=w["ln1"][:, 0:1]).then_inc(o1_ready, 1)
                b = it - 3
                if inside(b, BATCH):
                    act.wait_ge(h2_back, b + 1)
                    wait_free(act, cov_ready, b)
                    nc.scalar.activation(h2[:, q, :, 0:D], pXf[:], ACT.Copy).then_inc(h2_ready, 1)

            sweep(act, BATCH, 3, body)

        @block.tensor
        def _(pe):
            pe.wait_ge(init, 2)

            def turn(i, b, dst):
                pe.wait_ge(xn_ready[i], b + 1)
                for j in range(JT):
                    last = nc.tensor.transpose(dst[:, j * P:(j + 1) * P], xn[i][:, j, :], ident[:])
                last.then_inc(turned[i], 1)

            def body(it, par, pair):
                q = 1 - par
                b = it - 1
                if inside(b, BATCH):
                    pe.wait_ge(o1_ready, b + 1)
                    wait_free(pe, z_ready, b, per=FC, depth=1)
                    for f in range(FC):
                        last = nc.tensor.matmul(pF[:, f, :], w["w1"][:, f * P:(f + 1) * P], o1T[:, q, :], start=True, stop=True)
                    last.then_inc(f1_ready, 1)
                b = it - 2
                if inside(b, BATCH):
                    wait_free(pe, y_ready, b, depth=1)
                    turn(1, b, pA2)
                b = it - 3
                if inside(b, BATCH):
                    if inside(it - 1, BATCH):
                        pe.wait_ge(o1_ready, it)
                    turn(2, b, pA)
                b = it - 4
                if inside(b, BATCH):
                    pe.wait_ge(h2_ready, b + 1)
                    pe.wait_ge(cov_added, b + 1)
                    for j in range(JT):
                        last = nc.tensor.matmul(pC[:], h2[:, par, j, 0:D], h2[:, par, j, :], start=(j == 0), stop=(j == JT - 1))
                    last.then_inc(cov_ready, 1)
                b = it
                if inside(b, BATCH):
                    if inside(it - 3, BATCH):
                        pe.wait_ge(h2T_ready, it - 3 + 1)
                    turn(0, b, pA)
                b = it - 2
                if inside(b, BATCH):
                    pe.wait_ge(y_ready, b + 1)
                    wait_free(pe, xm_ready, b, depth=1)
                    for j in range(JT):
                        last = nc.tensor.transpose(pB[:, j, :], yT[:, j * P:(j + 1) * P], ident[:])
                    last.then_inc(y_back, 1)
                b = it - 1
                if inside(b, BATCH):
                    pe.wait_ge(hid_ready, b + 1)
                    wait_free(pe, xn_ready[1], b, depth=1)
                    for j in range(JT):
                        tok = slice(j * P, (j + 1) * P)
                        for f in range(FC):
                            nc.tensor.matmul(pX[:, j, :], hid[:, f, tok], w["w2"][:, f, :], start=(f == 0), stop=False)
                        nc.tensor.matmul(pX[:, j, :], w["ones"][0:1, :], w["b2"][0:1, :], start=False, stop=False)
                        last = nc.tensor.matmul(pX[:, j, :], o1T[:, q, tok], ident[:], start=False, stop=True)
                    last.then_inc(x2_ready, 1)
                b = it - 3
                if inside(b, BATCH):
                    pe.wait_ge(h2T_ready, b + 1)
                    wait_free(pe, h2_ready, b, depth=1)
                    for j in range(JT):
                        last = nc.tensor.transpose(pXf[:, j, :], h2T[:, q, j * P:(j + 1) * P], ident[:])
                    last.then_inc(h2_back, 1)

            sweep(pe, BATCH, 4, body)

        @block.sync
        def _(sp):
            def body(it, par, pair):
                b = it
                if inside(b, BATCH):
                    hold(sp, h2T_ready, b + 1)
                    wait_free(sp, h2T_saved, b, per=16, depth=1)
                    settle(sp)
                    sp.dma_start(w["h2T"][:, b, :], h2T[:, par, :]).then_inc(h2T_saved, 16)

            sweep(sp, BATCH, 0, body)
            sp.wait_ge(h2T_saved, 16 * BATCH)


def fold_phase(nc, w, io):
    with ExitStack() as ctx:
        t = Tools(nc, ctx, "fold")
        wq = t.sb("wq", [P, QB * P])
        wqT = t.sb("wqT", [P, QB, P])
        krow = t.sb("krow", [P, 4, P])
        keysT = t.sb("keysT", [P, PH, NK, 2])
        keysS = t.sb("keysS", [P, QB, NK])
        down = t.sb("down", [P, EB, P])
        grow = t.sb("grow", [QB, P])
        brow = t.sb("brow", [QB, P])
        gT = t.sb("gT", [P, QB])
        bT = t.sb("bT", [P, QB])
        cm = t.sb("cm", [P, D + 1])
        mrow = t.sb("mrow", [1, P])
        prod = t.sb("prod", [P, 3, P])
        var = t.sb("var", [P, QB])
        mean = t.sb("mean", [P, QB])
        var_e = t.sb("var_e", [P, QB])
        inv = t.sb("inv", [P, QB])
        s_ = t.sb("scale", [P, QB])
        sh = t.sb("shift", [P, QB])
        pa = [t.ps(f"pa{i}", [P, 4, P]) for i in range(2)]
        pc = [t.ps(f"pc{i}", [P, 3, D + 1]) for i in range(2)]
        pm = t.ps("pm", [P, 512])
        pw = t.ps("pw", [P, QB, NK])
        pb = t.ps("pb", [1, QB, NK])
        loaded, turned, turned_used = t.sem("loaded"), t.sem("turned"), t.sem("turned_used")
        vec, m_ready, m_turned, mm_ready, cm_ready = (t.sem(n) for n in ("vec", "m_ready", "m_turned", "mm_ready", "cm_ready"))
        q_ready, q_used, v_ready, ve_ready, inv_ready, keys_ready, sh_ready, w_ready = (
            t.sem(n) for n in ("q_ready", "q_used", "v_ready", "ve_ready", "inv_ready", "keys_ready", "sh_ready", "w_ready"))
        drawn = t.sem("drawn")
        block = ctx.enter_context(nc.Block())
        ident = w["ident"]
        blocks = [(krow[:, g, :], keysT[:].rearrange("p h k a -> p (h k a)")[:, g * P:(g + 1) * P]) for g in range(4)]
        blocks += [(down[:, g, :], w["downT"][:, g, :]) for g in range(EB)]
        blocks += [(wq[:, g * P:(g + 1) * P], wqT[:, g, :]) for g in range(QB)]
        NB = len(blocks) // 4
        dests = ([keysT[:].rearrange("p h k a -> p (h k a)").rearrange("p (g e) -> p g e", g=4)]
                 + [w["downT"][:, 4 * g:4 * g + 4, :] for g in range(EB // 4)]
                 + [wqT[:, 4 * g:4 * g + 4, :] for g in range(QB // 4)])
        qgroups = [list(range(g, min(g + 3, QB))) for g in range(0, QB, 3)]

        @block.sync
        def _(sp):
            for dst, src in (
                (krow[:], io["keys"].rearrange("h k a c -> (h k a) c").rearrange("(g r) c -> r g c", r=P)),
                (down[:], io["down"].rearrange("(g e) d -> e g d", e=P)),
                (wq[:], io["w_q"]),
                (w["up"][:], io["up"].rearrange("(g e) d -> e g d", e=P)),
                (grow[:], io["gamma"].rearrange("(g c) -> g c", c=P)),
                (brow[:], io["beta"].rearrange("(g c) -> g c", c=P)),
            ):
                sp.dma_start(dst, src).then_inc(loaded, 16)
            sp.wait_ge(loaded, 96)

        @block.gpsimd
        def _(pool):
            nc.gpsimd.iota(w["iotaE"][:], [[1, P], [0, HALF]], base=0, channel_multiplier=0,
                           allow_small_or_imprecise_dtypes=True).then_inc(drawn, 1)
            nc.gpsimd.iota(w["iota8"][:], [[1, EB], [0, HALF]], base=0, channel_multiplier=0,
                           allow_small_or_imprecise_dtypes=True).then_inc(drawn, 1)
            nc.gpsimd.iota(w["order"][:], [[0, PH], [-int(KEYB), CAND]], base=32 * int(KEYB), channel_multiplier=0,
                           allow_small_or_imprecise_dtypes=True).then_inc(drawn, 1)
            pool.wait_ge(ve_ready, 1)
            nc.gpsimd.tensor_tensor(inv[:], var_e[:], w["mhalf"][:], ALU.pow).then_inc(inv_ready, 1)
            pool.wait_ge(drawn, 3)

        @block.tensor
        def _(pe):
            pe.wait_ge(m_ready, 1)
            nc.tensor.transpose(pm[0:1, 0:P], cm[:, D:D + 1], ident[:]).then_inc(m_turned, 1)
            pe.wait_ge(m_ready, 2)
            nc.tensor.matmul(pm[:, P:2 * P], mrow[:], mrow[:], start=True, stop=True).then_inc(mm_ready, 1)
            pe.wait_ge(loaded, 96)
            pe.wait_ge(cm_ready, 1)
            nc.tensor.transpose(pm[:, 2 * P:2 * P + QB], grow[:], ident[0:QB, 0:QB])
            nc.tensor.transpose(pm[:, 3 * P:3 * P + QB], brow[:], ident[0:QB, 0:QB]).then_inc(mm_ready, 1)
            for k in range(NB):
                if k >= 2:
                    pe.wait_ge(turned_used, k - 1)
                for q in range(4):
                    last = nc.tensor.transpose(pa[k % 2][:, q, :], blocks[4 * k + q][0], ident[:])
                last.then_inc(turned, 1)
            for k, group in enumerate(qgroups):
                if k >= 2:
                    pe.wait_ge(q_used, k - 1)
                for i, g in enumerate(group):
                    last = nc.tensor.matmul(pc[k % 2][:, i, :], wq[:, g * P:(g + 1) * P], cm[:], start=True, stop=True)
                last.then_inc(q_ready, 1)
            pe.wait_ge(turned_used, NB)
            pe.wait_ge(keys_ready, 2)
            for g in range(QB):
                last = nc.tensor.matmul(pw[:, g, :], wqT[:, g, :], keysS[:, g, :], start=True, stop=True)
            last.then_inc(w_ready, 1)
            pe.wait_ge(sh_ready, 1)
            for g in range(QB):
                last = nc.tensor.matmul(pb[:, g, :], sh[:, g:g + 1], keysT[:, g % PH, :, g // PH], start=True, stop=True)
            last.then_inc(w_ready, 1)

        @block.vector
        def _(dve):
            c = Chain(dve, vec)
            n = 1.0 / (BATCH * SEQ)
            nc.vector.tensor_scalar(cm[:, D:D + 1], w["cov"][:, D:D + 1], n, None, MUL).then_inc(m_ready, 1)
            dve.wait_ge(m_turned, 1)
            nc.vector.tensor_copy(mrow[:], pm[0:1, 0:P]).then_inc(m_ready, 1)
            c.link(nc.vector.tensor_scalar(prod[:, 0, :], w["cov"][:, 0:D], n, None, MUL))
            c.wait()
            dve.wait_ge(mm_ready, 1)
            nc.vector.tensor_tensor(cm[:, 0:D], prod[:, 0, :], pm[:, P:2 * P], SUB).then_inc(cm_ready, 1)
            dve.wait_ge(mm_ready, 2)
            c.link(nc.vector.tensor_copy(gT[:], pm[:, 2 * P:2 * P + QB]))
            c.link(nc.vector.tensor_copy(bT[:], pm[:, 3 * P:3 * P + QB]))
            for k in range(NB):
                dve.wait_ge(turned, k + 1)
                nc.vector.tensor_copy(dests[k], pa[k % 2][:]).then_inc(turned_used, 1)
            dve.wait_ge(turned_used, NB)
            dve.wait_ge(cm_ready, 1)
            for k, group in enumerate(qgroups):
                m = len(group)
                g = group[0]
                dve.wait_ge(q_ready, k + 1)
                c.wait()
                c.link(nc.vector.tensor_tensor(prod[:, 0:m, :], pc[k % 2][:, 0:m, 0:D], wqT[:, g:g + m, :], MUL))
                nc.vector.tensor_copy(mean[:, g:g + m], pc[k % 2][:, 0:m, D]).then_inc(q_used, 1)
                c.wait()
                c.link(nc.vector.tensor_reduce(var[:, g:g + m], prod[:, 0:m, :], AX.X, ADD))
            c.wait()
            nc.vector.tensor_scalar(var_e[:], var[:], 0.0, EPS_BN, MAX, ADD).then_inc(ve_ready, 1)
            dve.wait_ge(inv_ready, 1)
            c.link(nc.vector.tensor_tensor(s_[:], gT[:], inv[:], MUL))
            c.wait()
            dve.wait_ge(q_used, len(qgroups))
            for a in range(2):
                nc.vector.tensor_tensor(keysS[:, a * PH:(a + 1) * PH, :], keysT[:, :, :, a], bc(s_[:, a * PH:(a + 1) * PH], 2, NK),
                                        MUL).then_inc(keys_ready, 1)
            c.link(nc.vector.tensor_tensor(mean[:], mean[:], s_[:], MUL))
            c.wait()
            nc.vector.tensor_tensor(sh[:], bT[:], mean[:], SUB).then_inc(sh_ready, 1)
            dve.wait_ge(w_ready, 2)
            nc.vector.tensor_copy(w["wkey"][:], pw[:].rearrange("p g k -> p (g k)"))
            nc.vector.tensor_copy(w["bkey"][:], pb[:].rearrange("p g k -> p (g k)"))


def experts_phase(nc, w, out):
    with ExitStack() as ctx:
        t = Tools(nc, ctx, "exp")
        C8 = CAND + TOPK
        h2c = t.sb("h2c", [P, 2, P])
        sims = t.sb("sims", [P, 2, QB, NK])
        sv = t.sb("sv", [P, QB, TOPK])
        si = t.sb("si", [P, 2, QB, TOPK], U16)
        row = t.sb("row", [P, PH, TOPK])
        col = t.sb("col", [P, PH, TOPK])
        cand = t.sb("cand", [P, PH, C8])
        ge = t.sb("ge", [P, 2, PH, CAND])
        rel = t.sb("rel", [P, 2, PH, C8])
        place = t.sb("place", [P, PH, CAND])
        pay = t.sb("pay", [P, 3, PH, CAND])
        zsum = t.sb("zsum", [P, 2, PH])
        rz = t.sb("rz", [P, 2, PH])
        wt = t.sb("wt", [P, PH, CAND])
        wr = t.sb("wr", [P, PH, CAND])
        keyv = t.sb("keyv", [P, 2, 3, PH, CAND])
        kept = t.sb("kept", [P, 3, PH, TOPK], U32)
        bits = t.sb("bits", [P, 4, PAIR], U32)
        half = t.sb("half", [P, 4, 2, PAIR], F16)
        pairs = t.sb("pairs", [P, 2, 4, HALF], F16)
        onee = t.sb("onee", [P, P, HALF], F16)
        oneb = t.sb("oneb", [P, EB, HALF], F16)
        wb = t.sb("wb", [P, 2, EB, 2, HALF], F16)
        act_e = t.sb("act_e", [P, EB, P])
        prod = t.sb("prod", [P, EB, P])
        yT = t.sb("yT", [P, P])
        xo = t.sb("xo", [P, 2, D])
        pS = t.ps("pS", [P, QB, NK])
        pT = t.ps("pT", [P, 4, P], F16)
        pW = [t.ps(f"pW{i}", [P, HALF // 2, EB, 2]) for i in range(2)]
        pG = t.ps("pG", [P, EB, P])
        pO = t.ps("pO", [P, 512])
        pF = t.ps("pF", [P, 512])
        h2_loaded = [t.sem(f"h2_loaded{i}") for i in range(2)]
        stored = [t.sem(f"stored{i}") for i in range(2)]
        names = ("sims_ready sims_kept best index cand_sum best8 flags rel_ready sum_ready rz_ready exp_ready rc_ready "
                 "pay_w pay_i place_ready keys_made packed masked half_ready turned pairs_ready one_ready oneb_ready wb_ready "
                 "w_ready g_ready gelu_ready prod_ready o_ready y_ready back xo_ready init pw_used").split()
        S = {n: t.sem(n) for n in names}
        block = ctx.enter_context(nc.Block())
        ident, ident16, mod = w["ident"], w["ident16"], w["mod"]
        starts = [sum(RANKS[:a]) for a in range(TOPK)]

        @block.sync
        def _(sp):
            o = out.rearrange("b (j p) d -> b j p d", p=P)

            def body(it, par, pair):
                n = it
                if inside(n, TILES):
                    wait_free(sp, S["sims_ready"], n)
                    sp.dma_start(h2c[:, par, :], w["h2T"][:, pair, par * P:(par + 1) * P]).then_inc(h2_loaded[par], 16)
                n, q = it - 5, 1 - par
                if inside(n, TILES):
                    hold(sp, S["xo_ready"], n + 1)
                    sp.dma_start(o[pair - 3 + par, q, :, :], xo[:, q, :]).then_inc(stored[q], 16)

            sweep(sp, TILES, 5, body)
            for p in range(2):
                sp.wait_ge(stored[p], 16 * (TILES // 2))

        @block.vector
        def _(dve):
            V = nc.vector
            V.memset(wb[:], 0.0).then_inc(S["init"], 1)
            dve.wait_ge(S["init"], 1)

            def best(n, par):
                dve.wait_ge(S["sims_kept"], n + 1)
                wait_free(dve, S["cand_sum"], n, per=4, depth=1)
                settle(dve)
                for g in range(QB):
                    V.max(sv[:, g, :], sims[:, par, g, :]).then_inc(S["best"], 1)
                wait_free(dve, S["rc_ready"], n, per=2)
                hold(dve, S["best"], (n + 1) * QB)
                for g in range(QB):
                    V.max_index(si[:, par, g, :], sv[:, g, :], sims[:, par, g, :]).then_inc(S["index"], 1)
                wait_free(dve, S["rel_ready"], n, depth=1)
                wait_free(dve, S["flags"], n, per=2, depth=1)
                sx, sy = sv[:, 0:PH, :], sv[:, PH:QB, :]
                sums(V.tensor_tensor, cand, sx, sy, S["cand_sum"])
                hold(dve, S["cand_sum"], (n + 1) * 4)
                for h in range(PH):
                    V.max(cand[:, h, CAND:C8], cand[:, h, 0:CAND]).then_inc(S["best8"], 1)
                hold(dve, S["best8"], (n + 1) * PH)
                wait_free(dve, S["place_ready"], n, depth=1)
                for k, op in enumerate((ALU.is_ge, ALU.is_gt)):
                    V.tensor_tensor(ge[:, k, :, :], cand[:, :, 0:CAND], bc(cand[:, :, C8 - 1], 2, CAND), op).then_inc(S["flags"], 1)
                wait_free(dve, S["pay_w"], n)
                V.tensor_tensor(rel[:, par, :, :], cand[:], bc(cand[:, :, CAND], 2, C8), SUB).then_inc(S["rel_ready"], 1)

            def sums(add, dst, sx, sy, sem):
                s = starts
                add(dst[:, :, 0:8], bc(sx[:, :, 0], 2, 8), sy[:, :, 0:8], ADD).then_inc(sem, 1)
                add(dst[:, :, s[1]:s[1] + 4], bc(sx[:, :, 1], 2, 4), sy[:, :, 0:4], ADD).then_inc(sem, 1)
                add(dst[:, :, s[2]:s[4]].rearrange("p h (a b) -> p h a b", b=2), bc(sx[:, :, 2:4], 3, 2), bc(sy[:, :, 0:2], 2, 2),
                    ADD).then_inc(sem, 1)
                add(dst[:, :, s[4]:s[4] + 4], sx[:, :, 4:8], bc(sy[:, :, 0], 2, 4), ADD).then_inc(sem, 1)

            def body(it, par, pair):
                q = 1 - par
                n = it
                if inside(n, TILES):
                    best(n, par)
                n = it - 4
                if inside(n, TILES):
                    dve.wait_ge(S["gelu_ready"], n + 1)
                    dve.wait_ge(S["w_ready"], n * 2 + 2)
                    wait_free(dve, S["o_ready"], n, depth=1)
                    for i in range(2):
                        tok = slice(i * HALF, (i + 1) * HALF)
                        V.tensor_tensor(prod[:, :, tok].rearrange("p e (t a) -> p e t a", a=2),
                                        pW[i][:].rearrange("p t e a -> p e t a"),
                                        act_e[:, :, tok].rearrange("p e (t a) -> p e t a", a=2), MUL).then_inc(S["prod_ready"], 1)
                n = it - 1
                if inside(n, TILES):
                    dve.wait_ge(S["exp_ready"], n + 1)
                    wait_free(dve, S["pay_w"], n)
                    V.tensor_reduce(zsum[:, q, :], rel[:, q, :, CAND:C8], AX.X, ADD).then_inc(S["sum_ready"], 1)
                    dve.wait_ge(S["sum_ready"], n + 1)
                    V.reciprocal(rz[:, q, :], zsum[:, q, :]).then_inc(S["rz_ready"], 1)
                n = it - 2
                if inside(n, TILES):
                    dve.wait_ge(S["keys_made"], n + 1)
                    wait_free(dve, S["masked"], n, per=3, depth=1)
                    settle(dve)
                    for f in range(3):
                        for h in range(PH):
                            V.max(kept[:, f, h, :], keyv[:, par, f, h, :]).then_inc(S["packed"], 1)
                    dve.wait_ge(S["packed"], (n + 1) * 3 * PH)
                    wait_free(dve, S["half_ready"], n, per=2, depth=1)
                    flat = kept[:].rearrange("p f h k -> p f (h k)")
                    V.tensor_scalar(bits[:, 0, :], flat[:, 0, :], P - 1, None, ALU.bitwise_and).then_inc(S["masked"], 1)
                    V.tensor_scalar(bits[:, 1, :], flat[:, 0, :], 7, EB - 1, ALU.logical_shift_right, ALU.bitwise_and).then_inc(S["masked"], 1)
                    V.tensor_scalar(bits[:, 2:4, :], flat[:, 1:3, :], int(KEYB) - 1, None, ALU.bitwise_and).then_inc(S["masked"], 1)
                n = it - 3
                if inside(n, TILES):
                    v = pairs[:, q, :, :]
                    dve.wait_ge(S["pairs_ready"], (n + 1) * 2)
                    wait_free(dve, S["w_ready"], n, per=2, depth=1)
                    wait_free(dve, S["wb_ready"], n, per=2, depth=1)
                    V.tensor_tensor(oneb[:], bc(v[:, 1, :], 1, EB), w["iota8"][:], ALU.is_equal).then_inc(S["oneb_ready"], 1)
                    V.tensor_tensor(onee[:], bc(v[:, 0, :], 1, P), w["iotaE"][:], ALU.is_equal).then_inc(S["one_ready"], 1)
                    dve.wait_ge(S["oneb_ready"], n + 1)
                    for a in range(2):
                        r = slice(a * PAIR, (a + 1) * PAIR)
                        V.tensor_tensor(wb[r, :, :, a, :], bc(oneb[r, :, :], 1, 2), bc(v[r, 2:4, :], 2, EB), MUL).then_inc(S["wb_ready"], 1)
                n = it - 5
                if inside(n, TILES):
                    dve.wait_ge(S["back"], n + 1)
                    if not isinstance(n, int) or n >= 2:
                        dve.wait_ge(stored[q], (pair - 3 + par) * 16)
                    V.tensor_tensor(xo[:, q, :], pF[:, 0:D], w["x"][:, n, :], ADD).then_inc(S["xo_ready"], 1)

            sweep(dve, TILES, 5, body)

        @block.gpsimd
        def _(pool):
            G = nc.gpsimd

            def body(it, par, pair):
                q = 1 - par
                n = it - 1
                if inside(n, TILES):
                    hold(pool, S["index"], (n + 1) * QB)
                    G.tensor_scalar(row[:], si[:, q, 0:PH, :], float(NK), None, MUL).then_inc(S["rc_ready"], 1)
                    G.tensor_scalar(col[:], si[:, q, PH:QB, :], 1.0, None, MUL).then_inc(S["rc_ready"], 1)
                    pool.wait_ge(S["rc_ready"], (n + 1) * 2)
                    s = starts
                    i_ = pay[:, 0, :, :]
                    wait_free(pool, S["keys_made"], n, depth=1)
                    G.tensor_tensor(i_[:, :, 0:8], bc(row[:, :, 0], 2, 8), col[:, :, 0:8], ADD).then_inc(S["pay_i"], 1)
                    G.tensor_tensor(i_[:, :, s[1]:s[1] + 4], bc(row[:, :, 1], 2, 4), col[:, :, 0:4], ADD).then_inc(S["pay_i"], 1)
                    G.tensor_tensor(i_[:, :, s[2]:s[2] + 2], bc(row[:, :, 2], 2, 2), col[:, :, 0:2], ADD).then_inc(S["pay_i"], 1)
                    G.tensor_tensor(i_[:, :, s[3]:s[3] + 2], bc(row[:, :, 3], 2, 2), col[:, :, 0:2], ADD).then_inc(S["pay_i"], 1)
                    G.tensor_tensor(i_[:, :, s[4]:s[4] + 4], row[:, :, 4:8], bc(col[:, :, 0], 2, 4), ADD).then_inc(S["pay_i"], 1)
                    hold(pool, S["flags"], (n + 1) * 2)
                    c = Chain(pool, S["init_pool"], n * 7)
                    c.link(G.tensor_scalar(place[:], ge[:, 1, :, :], 32 * KEYB, None, MUL))
                    c.wait()
                    c.link(G.tensor_tensor(place[:], place[:], w["order"][:], ADD))
                    c.wait()
                    G.tensor_tensor(place[:], place[:], ge[:, 0, :, :], MUL).then_inc(S["place_ready"], 1)
                    pool.wait_ge(S["rz_ready"], n + 1)
                    G.tensor_tensor(wt[:], rel[:, q, :, 0:CAND], bc(rz[:, q, :], 2, CAND), MUL).then_inc(S["pay_w"], 1)
                    hold(pool, S["pay_w"], n + 1)
                    c.link(G.tensor_scalar(wr[:], wt[:], WSCALE, RND, MUL, ADD))
                    c.link(G.tensor_scalar(wt[:], wt[:], WSCALE, None, MUL))
                    c.wait()
                    c.link(G.tensor_scalar(pay[:, 1, :, :], wr[:], RND, None, SUB))
                    c.wait()
                    c.link(G.tensor_tensor(wt[:], wt[:], pay[:, 1, :, :], SUB))
                    c.wait()
                    c.link(G.tensor_scalar(pay[:, 2, :, :], wt[:], 2 * WSCALE, WSCALE, MUL, ADD))
                    c.wait()
                    assert c.k == 7
                    pool.wait_ge(S["place_ready"], n + 1)
                    pool.wait_ge(S["pay_i"], (n + 1) * 5)
                    wait_free(pool, S["packed"], n, per=3 * PH)
                    G.tensor_tensor(keyv[:, q, :, :, :].rearrange("p f h c -> p f (h c)"), pay[:].rearrange("p f h c -> p f (h c)"),
                                    bc(place[:].rearrange("p h c -> p (h c)"), 1, 3), ADD).then_inc(S["keys_made"], 1)

            S["init_pool"] = t.sem("init_pool")
            sweep(pool, TILES, 1, body)

        @block.scalar
        def _(act):
            A = nc.scalar.activation

            def body(it, par, pair):
                q = 1 - par
                n = it
                if inside(n, TILES):
                    act.wait_ge(S["sims_ready"], n + 1)
                    wait_free(act, S["index"], n, per=QB)
                    A(sims[:, par, :, :], pS[:], ACT.Copy).then_inc(S["sims_kept"], 1)
                n = it - 2
                if inside(n, TILES):
                    act.wait_ge(S["masked"], (n + 1) * 3)
                    wait_free(act, S["turned"], n, depth=1)
                    A(half[:, 0:3, :, :].rearrange("p f d k -> p f d k"), bc(bits[:, 0:3, :], 2, 2), ACT.Copy).then_inc(S["half_ready"], 1)
                    A(half[:, 3, :, :], bc(bits[:, 3, :], 1, 2), ACT.Copy, bias=-0.5, scale=0.5 / WSCALE).then_inc(S["half_ready"], 1)
                    act.wait_ge(S["turned"], n + 1)
                    wait_free(act, S["one_ready"], n)
                    wait_free(act, S["wb_ready"], n, per=2)
                    for a in range(2):
                        r = slice(a * PAIR, (a + 1) * PAIR)
                        A(pairs[r, par, :, :], pT[r, :, :].rearrange("p f (t a) -> p a f t", a=2)[:, a, :, :], ACT.Copy).then_inc(S["pairs_ready"], 1)
                n = it - 4
                if inside(n, TILES):
                    act.wait_ge(S["o_ready"], n + 1)
                    wait_free(act, S["back"], n, depth=1)
                    settle(act)
                    b = pair - 2
                    A(yT[:], pO[:, 0:P], ACT.Copy, scale=mod[:, b, GB:GB + 1]).then_inc(S["y_ready"], 1)
                n = it
                if inside(n, TILES):
                    act.wait_ge(S["rel_ready"], n + 1)
                    A(rel[:, par, :, :], rel[:, par, :, :], ACT.Exp).then_inc(S["exp_ready"], 1)
                n = it - 3
                if inside(n, TILES):
                    act.wait_ge(S["g_ready"], n + 1)
                    wait_free(act, S["prod_ready"], n, per=2, depth=1)
                    A(act_e[:], pG[:], ACT.Gelu_apprx_tanh).then_inc(S["gelu_ready"], 1)

            sweep(act, TILES, 4, body)

        @block.tensor
        def _(pe):
            def body(it, par, pair):
                q = 1 - par
                n = it
                if inside(n, TILES):
                    pe.wait_ge(h2_loaded[par], pair * 16 + 16)
                    wait_free(pe, S["sims_kept"], n, depth=1)
                    nc.tensor.matmul(pS[:].rearrange("p g k -> p (g k)"), h2c[:, par, :], w["wkey"][:], start=True, stop=False)
                    nc.tensor.matmul(pS[:].rearrange("p g k -> p (g k)"), w["ones"][0:1, :], w["bkey"][:], start=False, stop=True).then_inc(S["sims_ready"], 1)
                n = it - 5
                if inside(n, TILES):
                    pe.wait_ge(S["y_ready"], n + 1)
                    wait_free(pe, S["xo_ready"], n, depth=1)
                    nc.tensor.transpose(pF[:, 0:D], yT[:], ident[:]).then_inc(S["back"], 1)
                n = it - 3
                if inside(n, TILES):
                    wait_free(pe, S["gelu_ready"], n, depth=1)
                    b, j = (pair - 2, 1) if par == 0 else (pair - 1, 0)
                    for e in range(EB):
                        last = nc.tensor.matmul(pG[:, e, :], w["downT"][:, e, :], w["h2T"][:, b, j * P:(j + 1) * P], start=True, stop=True)
                    last.then_inc(S["g_ready"], 1)
                n = it - 2
                if inside(n, TILES):
                    pe.wait_ge(S["half_ready"], (n + 1) * 2)
                    wait_free(pe, S["pairs_ready"], n, per=2, depth=1)
                    for f in range(4):
                        last = nc.tensor.transpose(pT[:, f, :], half[:, f, :, :].rearrange("p d k -> p (d k)"), ident16[:])
                    last.then_inc(S["turned"], 1)
                n = it - 4
                if inside(n, TILES):
                    pe.wait_ge(S["prod_ready"], (n + 1) * 2)
                    wait_free(pe, S["y_ready"], n, depth=1)
                    for e in range(EB):
                        last = nc.tensor.matmul(pO[:, 0:P], w["up"][:, e, :], prod[:, e, :], start=(e == 0), stop=(e == EB - 1))
                    last.then_inc(S["o_ready"], 1)
                n = it - 3
                if inside(n, TILES):
                    pe.wait_ge(S["one_ready"], n + 1)
                    pe.wait_ge(S["wb_ready"], (n + 1) * 2)
                    wait_free(pe, S["prod_ready"], n, per=2, depth=1)
                    for i in range(2):
                        for k in range(HALF // 2):
                            p = i * (HALF // 2) + k
                            for part in range(2):
                                last = nc.tensor.matmul(pW[i][:, k, :, :].rearrange("p e a -> p (e a)"), onee[:, :, p],
                                                        wb[:, part, :, :, p].rearrange("p e a -> p (e a)"),
                                                        start=(part == 0), stop=(part == 1))
                        last.then_inc(S["w_ready"], 1)

            sweep(pe, TILES, 5, body)


def build(nc, io, out):
    with ExitStack() as ctx:
        t = Tools(nc, ctx, "w")
        w = {}
        for name, shape, dt in (
            ("ident", [P, P], F32), ("ident16", [P, P], F16), ("ones", [P, P], F32), ("mhalf", [P, QB], F32), ("epsk", [P, 1], F32), ("x1", [P, TILES, D], F32),
            ("x", [P, TILES, D], F32), ("mod", [P, BATCH, NV], F32),
            ("w1", [P, DFF], F32), ("w2", [P, FC, D], F32), ("b1", [P, FC], F32), ("b2", [1, D], F32), ("ln1", [P, 2], F32),
        ):
            w[name] = t.sb(name, shape, dt)
        with ExitStack() as ctx2:
            t2 = Tools(nc, ctx2, "w")
            for name, shape in (
                ("hT", [P, BATCH, SEQ]), ("G", [P, BATCH, HM]), ("ksum", [P, BATCH, PAIRS]), ("hsum", [P, BATCH]), ("cmax", [P, BATCH]),
                ("WqP", [P, HM]), ("WkP", [P, HM]), ("Wvo", [P, HEADS * D]), ("Wq", [P, HM]), ("Wk", [P, HM]),
            ):
                w[name] = t2.sb(name, shape)
            setup(nc, w, io)
            keys_phase(nc, w, io)
            queries_phase(nc, w)
        with ExitStack() as ctx2:
            t2 = Tools(nc, ctx2, "w")
            for name, shape in (("h2T", [P, BATCH, SEQ]), ("cov", [P, D + 1])):
                w[name] = t2.sb(name, shape)
            ffn_phase(nc, w, io)
            for name, shape, dt in (
                ("up", [P, EB, D], F32), ("downT", [P, EB, P], F32), ("wkey", [P, QB * NK], F32), ("bkey", [1, QB * NK], F32),
                ("iotaE", [P, P, HALF], F16), ("iota8", [P, EB, HALF], F16), ("order", [P, PH, CAND], F32),
            ):
                w[name] = t2.sb(name, shape, dt)
            fold_phase(nc, w, io)
            experts_phase(nc, w, out)


_NAMES = {
    "x": "L0_attn_x", "Wq": "L0_attn_Wq", "Wk": "L0_attn_Wk", "Wv": "L0_attn_Wv", "Wo": "L0_attn_Wo", "proj": "L0_attn_proj",
    "W1": "L0_attn_W1", "b1": "L0_attn_b1", "W2": "L0_attn_W2", "b2": "L0_attn_b2",
    "ln1_g": "L0_attn_ln1_g", "ln1_b": "L0_attn_ln1_b", "ln2_g": "L0_attn_ln2_g", "ln2_b": "L0_attn_ln2_b",
    "w_q": "L0_ffn_w_q", "gamma": "L0_ffn_bn_gamma", "beta": "L0_ffn_bn_beta", "keys": "L0_ffn_keys",
    "down": "L0_ffn_down_embed", "up": "L0_ffn_up_embed", "c": "L0_c", "wmod": "L0_wmod",
}


def kernel(**inputs):
    import numpy as _np
    import concourse.bacc as _bacc
    from concourse import mybir as _mybir
    from concourse.bass_utils import run_bass_kernel_spmd as _run

    nc = _bacc.Bacc("TRN2", target_bir_lowering=False, num_devices=1)
    arrays, io = {}, {}
    for short, name in _NAMES.items():
        a = _np.ascontiguousarray(inputs[name])
        arrays[f"in_{name}"] = a
        io[short] = nc.dram_tensor(f"in_{name}", a.shape, _mybir.dt.from_np(a.dtype), kind="ExternalInput").ap()
    out = nc.dram_tensor("out", (BATCH, SEQ, D), _mybir.dt.float32, kind="ExternalOutput").ap()
    build(nc, io, out)
    return _run(nc, [arrays], core_ids=[0]).results[0]["out"]
```

```python
from contextlib import ExitStack

import concourse.bass as bass
from concourse import mybir

F32 = mybir.dt.float32
F16 = mybir.dt.float16
U16 = mybir.dt.uint16
U32 = mybir.dt.uint32
ALU = mybir.AluOpType
ACT = mybir.ActivationFunctionType
AX = mybir.AxisListType
ADD, SUB, MUL, MAX, MIN = ALU.add, ALU.subtract, ALU.mult, ALU.max, ALU.min

P = 128
BATCH, SEQ, D = 16, 256, 128
JT = SEQ // P
TILES = BATCH * JT
HEADS, DH, M = 16, 64, 64
HM = HEADS * M
PAIRS = HEADS // 2
DFF = 512
FC = DFF // P
EPS_KERN = 1e-6
EPS_LN_ATTN, EPS_LN, EPS_BN = 1e-6, 1e-5, 1e-5
DN = float(DH) ** -0.25
PH, NK, TOPK = 8, 32, 8
NE = NK * NK
EB = NE // P
QB = 2 * PH
RANKS = [TOPK // (a + 1) for a in range(TOPK)]
CAND = sum(RANKS)
PAIR = PH * TOPK
KEYB = 8192.0
HALF = P // 2
WSCALE = 2048.0
RND = 12582912.0

SA, CA1, GAG, GAB, SB, CB1, GB = range(7)
NV = 8


def sweep(eng, n, lag, body, ahead=0):
    head = (lag + 3) // 2 * 2
    end = head + (n - ahead - head) // 2 * 2
    for it in range(head):
        body(it, it % 2, it // 2)
    with eng.Fori(head // 2, end // 2) as pair:
        body(pair * 2, 0, pair)
        body(pair * 2 + 1, 1, pair)
    for it in range(end, n + lag):
        body(it, it % 2, it // 2)


def inside(idx, n):
    return not isinstance(idx, int) or 0 <= idx < n


def wait_free(eng, sem, idx, per=1, depth=2):
    if isinstance(idx, int) and idx < depth:
        return
    eng.wait_ge(sem, (idx - depth + 1) * per)


def settle(eng):
    eng.nop(nofuse=True)


def hold(eng, sem, value):
    eng.wait_ge(sem, value)
    settle(eng)


def bc(ap, axis, n):
    v = ap.unsqueeze(axis)
    shape = list(v.shape)
    shape[axis] = n
    return v.broadcast_to(shape)


class Tools:

    def __init__(self, nc, ctx, tag):
        self.nc, self.ctx, self.tag = nc, ctx, tag

    def sb(self, name, shape, dt=F32):
        return self.ctx.enter_context(self.nc.sbuf_tensor(f"{self.tag}_{name}", shape, dt))

    def ps(self, name, shape, dt=F32):
        return self.ctx.enter_context(self.nc.psum_tensor(f"{self.tag}_{name}", shape, dt))

    def sem(self, name):
        return self.ctx.enter_context(self.nc.semaphore(f"{self.tag}_{name}"))


class Chain:

    def __init__(self, eng, sem, base=0):
        self.eng, self.sem, self.base, self.k = eng, sem, base, 0

    def link(self, ins):
        self.k += 1
        ins.then_inc(self.sem, 1)
        return self.k

    def wait(self):
        hold(self.eng, self.sem, self.base + self.k)


def setup(nc, w, io):
    with ExitStack() as ctx:
        t = Tools(nc, ctx, "set")
        wraw = {"q": w["Wq"], "k": w["Wk"], "v": t.sb("raw_v", [P, HM])}
        wT = {n: t.sb(f"T_{n}", [P, PAIRS, P]) for n in "qkv"}
        wo = t.sb("wo", [P, PAIRS, P])
        proj = t.sb("proj", [P, P])
        projT = t.sb("projT", [P, P])
        crow = t.sb("crow", [BATCH, D])
        cT = t.sb("cT", [P, BATCH])
        cs = t.sb("cs", [P, 4, BATCH])
        wmod = t.sb("wmod", [P, 6 * D])
        ln2 = t.sb("ln2", [P, 2])
        gt = t.sb("gt", [P, 2, 4, BATCH])
        pa = [t.ps(f"pa{i}", [P, 4, P]) for i in range(2)]
        pc = t.ps("pc", [P, 512])
        pm = t.ps("pm", [P, 512])
        ident = w["ident"]
        loaded_x, loaded_w, loaded_late = t.sem("loaded_x"), t.sem("loaded_w"), t.sem("loaded_late")
        loaded_c = t.sem("loaded_c")
        made = t.sem("made")
        turned, turned_used = t.sem("turned"), t.sem("turned_used")
        c_ready, mod_done, act_e = t.sem("c_ready"), t.sem("mod_done"), t.sem("act_e")
        vec = t.sem("vec")
        block = ctx.enter_context(nc.Block())

        @block.sync
        def _(sp):
            for n in "qkv":
                sp.dma_start(wraw[n][:], io[f"W{n}"].rearrange("d h k -> d (h k)")).then_inc(loaded_w, 16)
            sp.dma_start(wo[:], io["Wo"].rearrange("(p a) k o -> (a k) p o", a=2)).then_inc(loaded_w, 16)
            sp.wait_ge(made, 1)
            for a in range(2):
                sp.dma_start(proj[a * M:(a + 1) * M, a * DH:(a + 1) * DH], io["proj"]).then_inc(loaded_w, 16)
            x = io["x"].rearrange("b (j p) d -> p (b j) d", p=P)
            for g in range(4):
                n = TILES // 4
                sp.dma_start(w["x"][:, g * n:(g + 1) * n, :], x[:, g * n:(g + 1) * n, :]).then_inc(loaded_x, 16)
            for s, v in ((loaded_x, 64), (loaded_w, 96)):
                sp.wait_ge(s, v)

        @block.scalar
        def _(act):
            act.dma_start(crow[:], io["c"]).then_inc(loaded_c, 16)
            act.dma_start(wmod[:], io["wmod"]).then_inc(loaded_c, 16)
            act.dma_start(ln2[:, 0:1], io["ln2_g"].rearrange("(d a) -> d a", a=1)).then_inc(loaded_c, 16)
            act.dma_start(ln2[:, 1:2], io["ln2_b"].rearrange("(d a) -> d a", a=1)).then_inc(loaded_c, 16)
            late = [
                (w["w1"][:], io["W1"]),
                (w["w2"][:], io["W2"].rearrange("(c f) d -> f c d", f=P)),
                (w["b1"][:], io["b1"].rearrange("(c f) -> f c", f=P)),
                (w["b2"][:], io["b2"].rearrange("(a d) -> a d", a=1)),
                (w["ln1"][:, 0:1], io["ln1_g"].rearrange("(d a) -> d a", a=1)),
                (w["ln1"][:, 1:2], io["ln1_b"].rearrange("(d a) -> d a", a=1)),
            ]
            for dst, src in late:
                act.dma_start(dst, src, allow_slow_non_contiguous=True).then_inc(loaded_late, 16)
            act.wait_ge(c_ready, 1)
            nc.scalar.activation(cs[:, 0, :], cT[:], ACT.Exp, scale=-1.0).then_inc(act_e, 1)
            act.wait_ge(loaded_late, 16 * len(late))

        @block.gpsimd
        def _(pool):
            nc.gpsimd.memset(proj[:], 0.0).then_inc(made, 1)
            nc.gpsimd.memset(ident[:], 0.0).then_inc(made, 1)
            nc.gpsimd.memset(w["ident16"][:], 0.0).then_inc(made, 1)
            nc.gpsimd.memset(w["ones"][:], 1.0).then_inc(made, 1)
            nc.gpsimd.memset(w["mhalf"][:], -0.5).then_inc(made, 1)
            pool.wait_ge(made, 5)
            for m in (ident, w["ident16"]):
                nc.gpsimd.affine_select(out=m[:], in_=m[:], compare_op=ALU.not_equal, fill=1.0, base=0,
                                        pattern=[[-1, P]], channel_multiplier=1).then_inc(made, 1)

        groups = [(n, g) for n in "qkv" for g in range(2)]

        @block.tensor
        def _(pe):
            pe.wait_ge(made, 7)
            pe.wait_ge(loaded_c, 64)
            nc.tensor.transpose(pc[:, 0:BATCH], crow[:], ident[0:BATCH, 0:BATCH]).then_inc(turned, 1)
            pe.wait_ge(loaded_w, 96)
            nc.tensor.transpose(pm[:, 0:P], proj[:], ident[:]).then_inc(turned, 1)
            for k, (n, g) in enumerate(groups):
                if k >= 2:
                    pe.wait_ge(turned_used, k - 1)
                for q in range(4):
                    p = 4 * g + q
                    last = nc.tensor.transpose(pa[k % 2][:, q, :], wraw[n][:, p * P:(p + 1) * P], ident[:])
                last.then_inc(turned, 1)
            pe.wait_ge(c_ready, 2)
            for s in range(6):
                last = nc.tensor.matmul(pm[:, s * BATCH:(s + 1) * BATCH], wmod[:, s * D:(s + 1) * D],
                                        cs[:, 3, :], start=True, stop=True)
            last.then_inc(mod_done, 1)
            k = len(groups)
            pe.wait_ge(turned_used, k)
            for n in "qk":
                for g in range(2):
                    pe.wait_ge(turned_used, k - 1)
                    for q in range(4):
                        last = nc.tensor.matmul(pa[k % 2][:, q, :], wT[n][:, 4 * g + q, :], projT[:], start=True, stop=True)
                    last.then_inc(turned, 1)
                    k += 1
            for g in range(4):
                pe.wait_ge(turned_used, k - 1)
                for q in range(4):
                    p = 4 * (g // 2) + q
                    r = slice((g % 2) * DH, (g % 2 + 1) * DH)
                    last = nc.tensor.matmul(pa[k % 2][:, q, :], wT["v"][r, p, :], wo[r, p, :], start=True, stop=True)
                last.then_inc(turned, 1)
                k += 1

        @block.vector
        def _(dve):
            c = Chain(dve, vec)
            dve.wait_ge(turned, 1)
            nc.vector.tensor_copy(cT[:], pc[:, 0:BATCH]).then_inc(c_ready, 1)
            dve.wait_ge(turned, 2)
            c.link(nc.vector.tensor_scalar(projT[:], pm[:, 0:P], DN, None, MUL))
            dve.wait_ge(act_e, 1)
            c.link(nc.vector.tensor_scalar(cs[:, 1, :], cs[:, 0, :], 1.0, None, ADD))
            c.wait()
            c.link(nc.vector.reciprocal(cs[:, 2, :], cs[:, 1, :]))
            c.wait()
            nc.vector.tensor_tensor(cs[:, 3, :], cs[:, 2, :], cT[:], MUL).then_inc(c_ready, 1)
            k = 2
            for n, g in groups:
                dve.wait_ge(turned, k + 1)
                nc.vector.tensor_copy(wT[n][:, 4 * g:4 * g + 4, :], pa[k % 2][:]).then_inc(turned_used, 1)
                k += 1
            dst = [w["WqP"][:, g * 512:(g + 1) * 512] for g in range(2)] + [w["WkP"][:, g * 512:(g + 1) * 512] for g in range(2)]
            wvo = w["Wvo"][:].rearrange("p (r a o) -> p a r o", a=2, o=D)
            dst = [d.rearrange("p (q o) -> p q o", q=4) for d in dst]
            dst += [wvo[:, g % 2, 4 * (g // 2):4 * (g // 2) + 4, :] for g in range(4)]
            for d in dst:
                dve.wait_ge(turned, k + 1)
                nc.vector.tensor_copy(d, pa[k % 2][:]).then_inc(turned_used, 1)
                k += 1
            dve.wait_ge(mod_done, 1)
            dve.wait_ge(loaded_c, 64)
            mod = w["mod"]
            pmv = pm[:, 0:6 * BATCH].rearrange("p (s b) -> p s b", s=6)
            for col, s in ((SA, 0), (SB, 3)):
                nc.vector.tensor_copy(mod[:, :, col], pmv[:, s, :])
            for col, s in ((CA1, 1), (CB1, 4)):
                nc.vector.tensor_scalar(mod[:, :, col], pmv[:, s, :], 1.0, None, ADD)
            for k, s in ((0, 2), (1, 5)):
                c.link(nc.vector.tensor_copy(gt[:, k, 0, :], pmv[:, s, :]))
            c.wait()
            for k in range(2):
                c.link(nc.vector.scalar_tensor_tensor(gt[:, k, 1, :], gt[:, k, 0, :], -1.0, gt[:, k, 0, :], MUL, MAX))
                c.link(nc.vector.tensor_scalar(gt[:, k, 2, :], gt[:, k, 0, :], 0.0, 2.0, ALU.is_ge, MUL))
            c.wait()
            for k in range(2):
                c.link(nc.vector.tensor_scalar(gt[:, k, 3, :], gt[:, k, 1, :], 0.25, None, MAX))
            c.wait()
            for k in range(2):
                c.link(nc.vector.scalar_tensor_tensor(gt[:, k, 0, :], gt[:, k, 2, :], -1.0, gt[:, k, 3, :], ADD, MUL))
            c.wait()
            nc.vector.tensor_scalar(mod[:, :, GAG], gt[:, 0, 0, :], ln2[:, 0:1], None, MUL)
            nc.vector.tensor_scalar(mod[:, :, GAB], gt[:, 0, 0, :], ln2[:, 1:2], None, MUL)
            nc.vector.tensor_scalar(mod[:, :, GB], gt[:, 1, 0, :], 1.0 / WSCALE, None, MUL)


def keys_phase(nc, w, io):
    with ExitStack() as ctx:
        t = Tools(nc, ctx, "key")
        st6 = t.sb("st6", [P, 2, JT, 6])
        mv = t.sb("mv", [P, 2, JT, 2])
        rs = t.sb("rs", [P, 2, JT])
        ve = t.sb("ve", [P, 2, JT])
        xn = t.sb("xn", [P, 2, JT, D])
        hT = t.sb("hT", [P, 2, SEQ])
        h = t.sb("h", [P, 2, JT, D])
        sq = t.sb("sq", [P, 2, 512])
        diag = t.sb("diag", [P, 2, HEADS // 2])
        arg = t.sb("arg", [P, 2, JT, HM])
        kfs = t.sb("kfs", [P, HM])
        rmax = t.sb("rmax", [P, 2, 2 * JT])
        bmax = t.sb("bmax", [P, 2, 1])
        cmax = t.sb("cmax", [P, 2, 1])
        ncmax = t.sb("ncmax", [P, 2, 1])
        pT = t.ps("pT", [P, 2, SEQ])
        pM = t.ps("pM", [P, 512])
        pK = [t.ps(f"pK{u}", [P, 512]) for u in range(2)]
        pD = [t.ps(f"pD{u}", [P, 512]) for u in range(2)]
        pG = [t.ps(f"pG{u}", [P, 512]) for u in range(2)]
        stats, var_e, rstd = t.sem("stats"), t.sem("var_e"), t.sem("rstd")
        agg = t.sem("agg")
        xn_ready, xT_ready, hT_ready, h_back, h_ready = (t.sem(n) for n in ("xn_ready", "xT_ready", "hT_ready", "h_back", "h_ready"))
        kfs_ready = t.sem("kfs_ready")
        hT_saved, hsum_done = t.sem("hT_saved"), t.sem("hsum_done")
        k_ready, k_squared, sq_summed = t.sem("k_ready"), t.sem("k_squared"), t.sem("sq_summed")
        dash_ready, dash_max, arg_ready = t.sem("dash_ready"), t.sem("dash_max"), t.sem("arg_ready")
        bmax_ready, cmax_ready, ncmax_ready, cmax_kept = (t.sem(n) for n in ("bmax_ready", "cmax_ready", "ncmax_ready", "cmax_kept"))
        kf_ready, g_ready, g_kept, ks_ready, ks_kept = (t.sem(n) for n in ("kf_ready", "g_ready", "g_kept", "ks_ready", "ks_kept"))
        block = ctx.enter_context(nc.Block())
        x, mod, ident = w["x"], w["mod"], w["ident"]

        @block.vector
        def _(dve):
            def body(it, par, pair):
                b, q = it - 1, 1 - par
                if inside(b, BATCH):
                    dve.wait_ge(rstd, b + 1)
                    wait_free(dve, xT_ready, b)
                    for j in range(JT):
                        nc.vector.tensor_scalar(xn[:, q, j, :], x[:, b * JT + j, :], mv[:, q, j, 0:1], rs[:, q, j:j + 1],
                                                SUB, MUL).then_inc(xn_ready, 1)
                b = it
                if inside(b, BATCH):
                    wait_free(dve, rstd, b)
                    wait_free(dve, xn_ready, b, per=JT)
                    settle(dve)
                    for j in range(JT):
                        nc.vector.bn_stats(st6[:, par, j, :], x[:, b * JT + j, :]).then_inc(stats, 1)
                    hold(dve, stats, (b + 1) * JT)
                    for j in range(JT):
                        nc.vector.bn_aggr(mv[:, par, j, :], st6[:, par, j, :]).then_inc(agg, 1)
                b = it - 2
                if inside(b, BATCH):
                    for j in range(JT):
                        for u in range(2):
                            n = (b * JT + j) * 2 + u
                            dve.wait_ge(k_squared, n + 1)
                            wait_free(dve, arg_ready, n)
                            nc.vector.tensor_reduce(diag[:, u, :], sq[:, u, :].rearrange("p (h k) -> p h k", k=DH),
                                                    AX.X, ADD).then_inc(sq_summed, 1)
                            dve.wait_ge(dash_ready, n + 1)
                            if j == 0 and u == 0:
                                wait_free(dve, bmax_ready, b)
                            nc.vector.tensor_reduce(rmax[:, par, 2 * j + u:2 * j + u + 1], pD[u][:], AX.X, MAX).then_inc(dash_max, 1)
                            dve.wait_ge(sq_summed, n + 1)
                            if j == 0 and u == 0:
                                wait_free(dve, kfs_ready, b)
                                wait_free(dve, g_ready, b, per=2)
                            nc.vector.tensor_tensor(
                                arg[:, par, j, u * 512:(u + 1) * 512].rearrange("p (h m) -> p h m", m=M),
                                pD[u][:].rearrange("p (h m) -> p h m", m=M), bc(diag[:, u, :], 2, M), SUB).then_inc(arg_ready, 1)
                    dve.wait_ge(dash_max, (b + 1) * 2 * JT)
                    wait_free(dve, cmax_ready, b)
                    nc.vector.tensor_reduce(bmax[:, par, :], rmax[:, par, :], AX.X, MAX).then_inc(bmax_ready, 1)
                b, q = it - 1, 1 - par
                if inside(b, BATCH):
                    dve.wait_ge(hT_ready, b + 1)
                    nc.vector.tensor_reduce(w["hsum"][:, bass.ds(b, 1)], hT[:, q, :], AX.X, ADD).then_inc(hsum_done, 1)
                b = it - 2
                if inside(b, BATCH):
                    dve.wait_ge(cmax_ready, b + 1)
                    wait_free(dve, kf_ready, b, per=JT)
                    nc.vector.tensor_scalar(ncmax[:, par, :], cmax[:, par, :], -1.0, None, MUL).then_inc(ncmax_ready, 1)
                    nc.vector.tensor_copy(w["cmax"][:, bass.ds(b, 1)], cmax[:, par, :]).then_inc(cmax_kept, 1)

            sweep(dve, BATCH, 2, body)

        @block.gpsimd
        def _(pool):
            def body(it, par, pair):
                b = it
                if inside(b, BATCH):
                    pool.wait_ge(agg, (b + 1) * JT)
                    wait_free(pool, xn_ready, b, per=JT)
                    settle(pool)
                    nc.gpsimd.tensor_scalar(ve[:, par, :], mv[:, par, :, 1], EPS_LN, None, ADD).then_inc(var_e, 1)
                    pool.wait_ge(var_e, b + 1)
                    nc.gpsimd.tensor_tensor(rs[:, par, :], ve[:, par, :], w["mhalf"][:, 0:JT], ALU.pow).then_inc(rstd, 1)
                b, q = it - 3, 1 - par
                if inside(b, BATCH):
                    pool.wait_ge(kf_ready, (b + 1) * JT)
                    wait_free(pool, ks_ready, b, depth=1)
                    nc.gpsimd.tensor_tensor(kfs[:], arg[:, q, 0, :], arg[:, q, 1, :], ADD).then_inc(kfs_ready, 1)
                b = it - 2
                if inside(b, BATCH):
                    pool.wait_ge(bmax_ready, b + 1)
                    wait_free(pool, ncmax_ready, b)
                    wait_free(pool, cmax_kept, b)
                    settle(pool)
                    nc.gpsimd.partition_all_reduce(cmax[:, par, :], bmax[:, par, :], P, bass.bass_isa.ReduceOp.max).then_inc(cmax_ready, 1)

            sweep(pool, BATCH, 3, body)

        @block.tensor
        def _(pe):
            def project(b, par, j):
                tok = hT[:, par, j * P:(j + 1) * P]
                for u in range(2):
                    n = (b * JT + j) * 2 + u
                    wait_free(pe, k_squared, n)
                    nc.tensor.matmul(pK[u][:], tok, w["Wk"][:, u * 512:(u + 1) * 512], start=True, stop=True).then_inc(k_ready, 1)
                    wait_free(pe, arg_ready, n)
                    nc.tensor.matmul(pD[u][:], tok, w["WkP"][:, u * 512:(u + 1) * 512], start=True, stop=True).then_inc(dash_ready, 1)

            def sums(b, q, u):
                wait_free(pe, g_kept, b * 2 + u)
                for j in range(JT):
                    last = nc.tensor.matmul(pG[u][:], h[:, q, j, :], arg[:, q, j, u * 512:(u + 1) * 512],
                                            start=(j == 0), stop=(j == JT - 1))
                last.then_inc(g_ready, 1)

            def body(it, par, pair):
                if inside(it - 2, BATCH):
                    project(it - 2, par, 0)
                b, q = it - 1, 1 - par
                if inside(b, BATCH):
                    wait_free(pe, h_ready, b, depth=1)
                    for i in range(JT):
                        pe.wait_ge(xn_ready, b * JT + i + 1)
                        last = nc.tensor.transpose(pT[:, 0, i * P:(i + 1) * P], xn[:, q, i, :], ident[:])
                    last.then_inc(xT_ready, 1)
                b, q = it - 3, 1 - par
                if inside(b, BATCH):
                    pe.wait_ge(kf_ready, (b + 1) * JT)
                    sums(b, q, 0)
                if inside(it - 2, BATCH):
                    project(it - 2, par, 1)
                if inside(b, BATCH):
                    sums(b, q, 1)
                    pe.wait_ge(kfs_ready, b + 1)
                    wait_free(pe, ks_kept, b, depth=1)
                    for p in range(PAIRS):
                        last = nc.tensor.matmul(pM[:, p:p + 1], kfs[:, p * P:(p + 1) * P], w["ones"][:, 0:1], start=True, stop=True)
                    last.then_inc(ks_ready, 1)
                b, q = it - 1, 1 - par
                if inside(b, BATCH):
                    pe.wait_ge(hT_ready, b + 1)
                    for j in range(JT):
                        last = nc.tensor.transpose(pT[:, 1, j * P:(j + 1) * P], hT[:, q, j * P:(j + 1) * P], ident[:])
                    last.then_inc(h_back, 1)

            sweep(pe, BATCH, 3, body)

        @block.scalar
        def _(act):
            def body(it, par, pair):
                b, q = it - 3, 1 - par
                if inside(b, BATCH):
                    act.wait_ge(ncmax_ready, b + 1)
                    act.wait_ge(arg_ready, (b + 1) * 2 * JT)
                    for j in range(JT):
                        nc.scalar.activation(arg[:, q, j, :], arg[:, q, j, :], ACT.Exp, bias=ncmax[:, q, :]).then_inc(kf_ready, 1)
                for j in range(JT):
                    b = it - 2
                    if inside(b, BATCH):
                        for u in range(2):
                            n = (b * JT + j) * 2 + u
                            act.wait_ge(k_ready, n + 1)
                            wait_free(act, sq_summed, n)
                            nc.scalar.activation(sq[:, u, :], pK[u][:], ACT.Square, scale=DN * 0.5 ** 0.5).then_inc(k_squared, 1)
                    b, q = it - 1, 1 - par
                    if j == 0 and inside(b, BATCH):
                        act.wait_ge(xT_ready, b + 1)
                        wait_free(act, dash_ready, b, per=2 * JT)
                        wait_free(act, h_back, b)
                        wait_free(act, hT_saved, b, per=16)
                        wait_free(act, hsum_done, b)
                        nc.scalar.activation(hT[:, q, :], pT[:, 0, :], ACT.Identity, bias=mod[:, b, SA:SA + 1],
                                             scale=mod[:, b, CA1:CA1 + 1]).then_inc(hT_ready, 1)
                b = it - 3
                if inside(b, BATCH):
                    for u in range(2):
                        act.wait_ge(g_ready, b * 2 + u + 1)
                        nc.scalar.activation(w["G"][:, b, u * 512:(u + 1) * 512], pG[u][:], ACT.Copy).then_inc(g_kept, 1)
                    act.wait_ge(ks_ready, b + 1)
                    nc.scalar.activation(w["ksum"][:, b, :], pM[:, 0:PAIRS], ACT.Copy).then_inc(ks_kept, 1)
                b, q = it - 1, 1 - par
                if inside(b, BATCH):
                    act.wait_ge(h_back, b + 1)
                    wait_free(act, g_ready, b, per=2)
                    nc.scalar.activation(h[:, q, :, :], pT[:, 1, :].rearrange("p (j d) -> p j d", j=JT), ACT.Copy).then_inc(h_ready, 1)

            sweep(act, BATCH, 3, body)

        @block.sync
        def _(sp):
            def body(it, par, pair):
                b = it
                if inside(b, BATCH):
                    hold(sp, hT_ready, b + 1)
                    wait_free(sp, hT_saved, b, per=16, depth=1)
                    settle(sp)
                    sp.dma_start(w["hT"][:, b, :], hT[:, par, :]).then_inc(hT_saved, 16)

            sweep(sp, BATCH, 0, body)
            sp.wait_ge(hT_saved, 16 * BATCH)


def queries_phase(nc, w):
    with ExitStack() as ctx:
        t = Tools(nc, ctx, "qry")
        gmax = t.sb("gmax", [P, 2])
        sc = t.sb("sc", [P, BATCH])
        ks = t.sb("ks", [P, BATCH, PAIRS])
        kdiag = t.sb("kdiag", [P, PAIRS, P])
        ksb = t.sb("ksb", [P, HM])
        weigh = t.sb("weigh", [P, HEADS, M + 1])
        kst = t.sb("kst", [P, BATCH, HEADS])
        den = t.sb("den", [P, HEADS])
        ehs = t.sb("ehs", [P, BATCH])
        gs = t.sb("gs", [P, HM])
        kv = t.sb("kv", [P, PAIRS, D])
        hTq = t.sb("hTq", [P, 2, P])
        hTr = t.sb("hTr", [P, 2, P])
        sq = t.sb("sq", [P, 2, 512])
        diag = t.sb("diag", [P, 2, HEADS // 2])
        hmax = t.sb("hmax", [P, 2, HEADS // 2])
        off = t.sb("off", [P, 2, HEADS // 2])
        qf = t.sb("qf", [P, 2, HM])
        rden = t.sb("rden", [P, HEADS])
        qn = t.sb("qn", [P, 2, HM])
        qnT = t.sb("qnT", [P, PAIRS, P])
        pK = [t.ps(f"pK{u}", [P, 512]) for u in range(2)]
        pD = [t.ps(f"pD{u}", [P, 512]) for u in range(2)]
        pE = [t.ps(f"pE{u}", [P, 4, P]) for u in range(2)]
        pS = t.ps("pS", [P, 512])
        pO = t.ps("pO", [P, 512])
        pre, pre_a, tot_ready = t.sem("pre"), t.sem("pre_a"), t.sem("tot_ready")
        hq_loaded = [t.sem(f"hq_loaded{i}") for i in range(2)]
        hr_loaded = [t.sem(f"hr_loaded{i}") for i in range(2)]
        (q_ready, q_squared, sq_summed, dash_ready, dash_max, off_ready, arg_ready, exp_ready) = (
            t.sem(n) for n in ("q_ready", "q_squared", "sq_summed", "dash_ready", "dash_max", "off_ready", "arg_ready", "exp_ready"))
        (kdiag_ready, kb_ready, kb_kept, weighed, den_ready, rden_ready, qn_ready, qn_turned, qn_kept) = (
            t.sem(n) for n in ("kdiag_ready", "kb_ready", "kb_kept", "weighed", "den_ready", "rden_ready", "qn_ready", "qn_turned", "qn_kept"))
        (gs_ready, kv_ready, kv_kept, out_ready, out_kept) = (
            t.sem(n) for n in ("gs_ready", "kv_ready", "kv_kept", "out_ready", "out_kept"))
        block = ctx.enter_context(nc.Block())
        ident = w["ident"]
        ksd = weigh[:].rearrange("p h m -> p (h m)")[:, 0:2 * BATCH * PAIRS].rearrange("p (k a) -> p k a", a=2)

        @block.sync
        def _(sp):
            def body(it, par, pair):
                if inside(it, TILES):
                    wait_free(sp, dash_ready, it, per=2)
                    sp.dma_start(hTq[:, par, :], w["hT"][:, pair, par * P:(par + 1) * P]).then_inc(hq_loaded[par], 16)
                n = it - 2
                if inside(n, TILES):
                    wait_free(sp, out_ready, n)
                    sp.dma_start(hTr[:, par, :], w["hT"][:, pair - 1, par * P:(par + 1) * P]).then_inc(hr_loaded[par], 16)

            sweep(sp, TILES, 2, body)

        @block.vector
        def _(dve):
            c = Chain(dve, pre)
            c.link(nc.vector.tensor_reduce(gmax[:, 0:1], w["cmax"][:], AX.X, MAX))
            nc.vector.tensor_scalar(ehs[:], w["hsum"][:], EPS_KERN, None, MUL)
            c.wait()
            c.link(nc.vector.tensor_scalar(gmax[:, 1:2], gmax[:, 0:1], -1.0, None, MUL))
            dve.wait_ge(pre_a, 1)
            c.link(nc.vector.tensor_tensor(ks[:], w["ksum"][:], bc(sc[:], 2, PAIRS), MUL))
            c.wait()
            c.link(nc.vector.tensor_scalar(ks[:], ks[:], SEQ * EPS_KERN, None, ADD))

            c.link(nc.vector.memset(ksd, 0.0))
            c.wait()
            for a in range(2):
                r = slice(a * M, (a + 1) * M)
                c.link(nc.vector.tensor_copy(ksd[r, :, a], ks[r, :, :].rearrange("p b q -> p (b q)")))
            dve.wait_ge(tot_ready, 1)
            c.link(nc.vector.tensor_scalar(kst[:].rearrange("p b h -> p (b h)"), pS[:, 0:BATCH * HEADS], EPS_KERN, None, MUL))

            def features(n, par, u):
                k = n * 2 + u
                heads = qf[:, par, u * 512:(u + 1) * 512].rearrange("p (h m) -> p h m", m=M)
                dve.wait_ge(dash_ready, k + 1)
                wait_free(dve, off_ready, k)
                nc.vector.tensor_reduce(hmax[:, u, :], pD[u][:].rearrange("p (h m) -> p h m", m=M), AX.X, MAX).then_inc(dash_max, 1)
                dve.wait_ge(q_squared, k + 1)
                wait_free(dve, off_ready, k)
                nc.vector.tensor_reduce(diag[:, u, :], sq[:, u, :].rearrange("p (h k) -> p h k", k=DH), AX.X, ADD).then_inc(sq_summed, 1)
                dve.wait_ge(sq_summed, k + 1)
                dve.wait_ge(dash_max, k + 1)
                wait_free(dve, arg_ready, k)
                nc.vector.tensor_tensor(off[:, u, :], hmax[:, u, :], diag[:, u, :], ADD).then_inc(off_ready, 1)
                dve.wait_ge(off_ready, k + 1)
                wait_free(dve, weighed, n)
                wait_free(dve, qn_ready, n)
                nc.vector.tensor_tensor(heads, pD[u][:].rearrange("p (h m) -> p h m", m=M), bc(off[:, u, :], 2, M), SUB).then_inc(arg_ready, 1)

            def body(it, par, pair):
                n = it
                if inside(n, TILES):
                    features(n, par, 0)
                if par == 1 and inside(pair, BATCH):
                    wait_free(dve, kv_ready, pair, per=2, depth=1)
                    nc.vector.tensor_scalar(gs[:], w["G"][:, pair, :], sc[:, bass.ds(pair, 1)], ehs[:, bass.ds(pair, 1)],
                                            MUL, ADD).then_inc(gs_ready, 1)
                n, q = it - 1, 1 - par
                if inside(n, TILES):
                    dve.wait_ge(weighed, n + 1)
                    wait_free(dve, rden_ready, n, depth=1)
                    nc.vector.tensor_reduce(den[:], weigh[:], AX.X, ADD).then_inc(den_ready, 1)
                    wait_free(dve, qn_ready, n, depth=1)
                    dve.wait_ge(den_ready, n + 1)
                    nc.vector.reciprocal(rden[:], den[:]).then_inc(rden_ready, 1)
                    dve.wait_ge(rden_ready, n + 1)
                    wait_free(dve, qn_turned, n, per=2)
                    nc.vector.scalar_tensor_tensor(qn[:, q, :].rearrange("p (h m) -> p h m", m=M),
                                                   qf[:, q, :].rearrange("p (h m) -> p h m", m=M), EPS_KERN,
                                                   bc(rden[:], 2, M), ADD, MUL).then_inc(qn_ready, 1)
                if inside(it, TILES):
                    features(it, par, 1)

            sweep(dve, TILES, 1, body)

        @block.gpsimd
        def _(pool):
            pool.wait_ge(pre, 8)

            def body(it, par, pair):
                n, q, b = it - 1, 1 - par, pair if par == 1 else pair - 1
                if inside(n, TILES):
                    pool.wait_ge(exp_ready, n * 2 + 2)
                    pool.wait_ge(kb_kept, b * 3 + 3)
                    wait_free(pool, den_ready, n, depth=1)
                    nc.gpsimd.tensor_tensor(weigh[:, :, 0:M], qf[:, q, :].rearrange("p (h m) -> p h m", m=M),
                                            ksb[:].rearrange("p (h m) -> p h m", m=M), MUL).then_inc(weighed, 1)
                if par == 0 and inside(pair, BATCH):
                    wait_free(pool, kb_ready, pair, per=2, depth=1)
                    settle(pool)
                    nc.gpsimd.tensor_tensor(kdiag[:], bc(ident[:], 1, PAIRS), bc(ks[:, pair, :], 2, P), MUL).then_inc(kdiag_ready, 1)

            sweep(pool, TILES, 1, body)

        @block.scalar
        def _(act):
            act.wait_ge(pre, 2)
            nc.scalar.activation(sc[:], w["cmax"][:], ACT.Exp, bias=gmax[:, 1:2]).then_inc(pre_a, 1)

            def square(n, u):
                k = n * 2 + u
                act.wait_ge(q_ready, k + 1)
                wait_free(act, sq_summed, k)
                nc.scalar.activation(sq[:, u, :], pK[u][:], ACT.Square, scale=DN * 0.5 ** 0.5).then_inc(q_squared, 1)

            def exp(n, par, u):
                act.wait_ge(arg_ready, n * 2 + u + 1)
                half = qf[:, par, u * 512:(u + 1) * 512]
                nc.scalar.activation(half, half, ACT.Exp).then_inc(exp_ready, 1)

            def body(it, par, pair):
                if inside(it, TILES):
                    square(it, 0)
                n = it - 2
                if inside(n, TILES):
                    for u in range(2):
                        act.wait_ge(qn_turned, n * 2 + u + 1)
                        wait_free(act, out_ready, n, depth=1)
                        nc.scalar.activation(qnT[:, 4 * u:4 * u + 4, :], pE[u][:], ACT.Copy).then_inc(qn_kept, 1)
                if inside(it, TILES):
                    square(it, 1)
                    exp(it, par, 0)
                if inside(n, TILES):
                    act.wait_ge(out_ready, n + 1)
                    nc.scalar.activation(w["x1"][:, n, :], pO[:, 0:D], ACT.Copy).then_inc(out_kept, 1)
                if par == 0 and inside(pair, BATCH):
                    if inside(it - 1, TILES):
                        act.wait_ge(den_ready, pair * 2)
                    else:
                        act.wait_ge(pre, 8)
                    nc.scalar.activation(weigh[:, :, M], kst[:, pair, :], ACT.Copy).then_inc(kb_kept, 1)
                    for u, src in enumerate((pS, pO)):
                        act.wait_ge(kb_ready, pair * 2 + u + 1)
                        if inside(it - 1, TILES):
                            act.wait_ge(weighed, pair * 2)
                        nc.scalar.activation(ksb[:, u * 512:(u + 1) * 512], src[:], ACT.Copy).then_inc(kb_kept, 1)
                if par == 1 and inside(pair, BATCH):
                    for u in range(2):
                        act.wait_ge(kv_ready, pair * 2 + u + 1)
                        wait_free(act, out_ready, pair, per=2, depth=1)
                        nc.scalar.activation(kv[:, 4 * u:4 * u + 4, :], pE[u][:], ACT.Copy).then_inc(kv_kept, 1)
                if inside(it, TILES):
                    exp(it, par, 1)

            sweep(act, TILES, 2, body)

        @block.tensor
        def _(pe):
            pe.wait_ge(pre, 7)
            nc.tensor.matmul(pS[:, 0:BATCH * HEADS], w["ones"][:], ksd.rearrange("p k a -> p (k a)"), start=True, stop=True).then_inc(tot_ready, 1)
            def project(n, par, pair, u):
                k = n * 2 + u
                if u == 0:
                    pe.wait_ge(hq_loaded[par], pair * 16 + 16)
                wait_free(pe, q_squared, k)
                nc.tensor.matmul(pK[u][:], hTq[:, par, :], w["Wq"][:, u * 512:(u + 1) * 512], start=True, stop=True).then_inc(q_ready, 1)
                wait_free(pe, arg_ready, k)
                nc.tensor.matmul(pD[u][:], hTq[:, par, :], w["WqP"][:, u * 512:(u + 1) * 512], start=True, stop=True).then_inc(dash_ready, 1)

            def body(it, par, pair):
                if inside(it, TILES):
                    project(it, par, pair, 0)
                n = it - 2
                if inside(n, TILES):
                    pe.wait_ge(qn_ready, n + 1)
                    for u in range(2):
                        if par == 0:
                            pe.wait_ge(kv_kept, (pair - 1) * 2 + u + 1)
                        else:
                            pe.wait_ge(qn_kept, (n - 1) * 2 + u + 1)
                        for q in range(4):
                            p = 4 * u + q
                            last = nc.tensor.transpose(pE[u][:, q, :], qn[:, par, p * P:(p + 1) * P], ident[:])
                        last.then_inc(qn_turned, 1)
                if inside(it, TILES):
                    project(it, par, pair, 1)
                if inside(n, TILES):
                    pe.wait_ge(qn_kept, n * 2 + 2)
                    pe.wait_ge(hr_loaded[par], pair * 16)
                    pe.wait_ge(kv_kept, (pair - 1) * 2 + 2)
                    wait_free(pe, out_kept, n, depth=1)
                    if par == 1 and inside(pair, BATCH):
                        pe.wait_ge(kb_kept, pair * 3 + 3)
                    for p in range(PAIRS):
                        nc.tensor.matmul(pO[:, 0:D], qnT[:, p, :], kv[:, p, :], start=(p == 0), stop=False)
                    nc.tensor.matmul(pO[:, 0:D], hTr[:, par, :], ident[:], start=False, stop=True).then_inc(out_ready, 1)
                if par == 0 and inside(pair, BATCH):
                    pe.wait_ge(kdiag_ready, pair + 1)
                    wait_free(pe, kb_kept, pair, per=3, depth=1)
                    for u, dst in enumerate((pS, pO)):
                        if u == 1 and inside(n, TILES):
                            pe.wait_ge(out_kept, n + 1)
                        nc.tensor.matmul(dst[:], w["ones"][:], kdiag[:, 4 * u:4 * u + 4, :].rearrange("p q m -> p (q m)"),
                                         start=True, stop=True).then_inc(kb_ready, 1)
                if par == 1 and inside(pair, BATCH):
                    pe.wait_ge(gs_ready, pair + 1)
                    for u in range(2):
                        if inside(n, TILES):
                            pe.wait_ge(qn_kept, n * 2 + u + 1)
                        for q in range(4):
                            for a in range(2):
                                h = 2 * (4 * u + q) + a
                                last = nc.tensor.matmul(pE[u][a * M:(a + 1) * M, q, :], gs[:, h * M:(h + 1) * M],
                                                        w["Wvo"][:, h * D:(h + 1) * D], start=True, stop=True)
                        last.then_inc(kv_ready, 1)

            sweep(pe, TILES, 2, body)


def ffn_phase(nc, w, io):
    with ExitStack() as ctx:
        t = Tools(nc, ctx, "ffn")
        st6 = [t.sb(f"st6{i}", [P, JT, 6]) for i in range(3)]
        mv = [t.sb(f"mv{i}", [P, 2, JT, 2]) for i in range(3)]
        ve = [t.sb(f"ve{i}", [P, JT]) for i in range(3)]
        rs = [t.sb(f"rs{i}", [P, 2, JT]) for i in range(3)]
        xn = [t.sb(f"xn{i}", [P, JT, D]) for i in range(3)]
        o1T = t.sb("o1T", [P, 2, SEQ])
        z = t.sb("z", [P, FC, SEQ])
        ez = t.sb("ez", [P, FC, SEQ])
        hid = t.sb("hid", [P, 2, FC, SEQ])
        yT = t.sb("yT", [P, SEQ])
        h2T = t.sb("h2T", [P, 2, SEQ])
        h2 = t.sb("h2", [P, 2, JT, D + 1])
        pF = t.ps("pF", [P, FC, SEQ])
        pA = t.ps("pA", [P, 512])
        pA2 = t.ps("pA2", [P, 512])
        pX = t.ps("pX", [P, JT, D])
        pXf = t.ps("pXf", [P, JT, D])
        pB = t.ps("pB", [P, JT, D])
        pC = t.ps("pC", [P, D + 1])
        stats = [t.sem(f"stats{i}") for i in range(3)]
        agg = [t.sem(f"agg{i}") for i in range(3)]
        vard = [t.sem(f"vard{i}") for i in range(3)]
        rstd = [t.sem(f"rstd{i}") for i in range(3)]
        xn_ready = [t.sem(f"xn_ready{i}") for i in range(3)]
        turned = [t.sem(f"turned{i}") for i in range(3)]
        o1_ready, y_ready, h2T_ready = t.sem("o1_ready"), t.sem("y_ready"), t.sem("h2T_ready")
        f1_ready, z_ready, min_ready, e_ready, hid_ready = (t.sem(n) for n in ("f1_ready", "z_ready", "min_ready", "e_ready", "hid_ready"))
        x2_ready, y_back, xm_ready, h2_back, h2_ready = (t.sem(n) for n in ("x2_ready", "y_back", "xm_ready", "h2_back", "h2_ready"))
        cov_ready, cov_added, h2T_saved = t.sem("cov_ready"), t.sem("cov_added"), t.sem("h2T_saved")
        init, loaded = t.sem("init"), t.sem("loaded")
        block = ctx.enter_context(nc.Block())
        ident, mod = w["ident"], w["mod"]
        EPS = (EPS_LN_ATTN, EPS_LN_ATTN, EPS_LN)

        @block.vector
        def _(dve):
            nc.vector.memset(w["cov"][:], 0.0).then_inc(cov_added, 1)
            for k in range(2):
                nc.vector.memset(h2[:, k, :, D:D + 1], 1.0).then_inc(init, 1)

            def statistics(i, b, par, src):
                wait_free(dve, vard[i], b)
                if i != 1:
                    wait_free(dve, xn_ready[i], b)
                settle(dve)
                for j in range(JT):
                    nc.vector.bn_stats(st6[i][:, j, :], src(j)).then_inc(stats[i], 1)
                hold(dve, stats[i], (b + 1) * JT)
                for j in range(JT):
                    nc.vector.bn_aggr(mv[i][:, par, j, :], st6[i][:, j, :]).then_inc(agg[i], 1)

            def normalise(i, b, par, src):
                dve.wait_ge(rstd[i], b + 1)
                wait_free(dve, turned[i], b, depth=1)
                for j in range(JT):
                    last = nc.vector.tensor_scalar(xn[i][:, j, :], src(j), mv[i][:, par, j, 0:1], rs[i][:, par, j:j + 1], SUB, MUL)
                last.then_inc(xn_ready[i], 1)

            def body(it, par, pair):
                q = 1 - par
                b = it - 3
                if inside(b, BATCH):
                    normalise(1, b, q, lambda j: pX[:, j, :])
                b = it - 4
                if inside(b, BATCH):
                    normalise(2, b, par, lambda j: w["x"][:, b * JT + j, :])
                b = it
                if inside(b, BATCH):
                    normalise(0, b, par, lambda j: w["x1"][:, b * JT + j, :])
                b = it - 1
                if inside(b, BATCH):
                    dve.wait_ge(z_ready, (b + 1) * FC)
                    wait_free(dve, hid_ready, b, depth=1)
                    nc.vector.tensor_scalar(ez[:], z[:], 0.0, None, MIN).then_inc(min_ready, 1)
                b = it - 5
                if inside(b, BATCH):
                    dve.wait_ge(cov_ready, b + 1)
                    dve.wait_ge(cov_added, b + 1)
                    nc.vector.tensor_tensor(w["cov"][:], pC[:], w["cov"][:], ADD).then_inc(cov_added, 1)
                b = it - 1
                if inside(b, BATCH):
                    dve.wait_ge(e_ready, b + 1)
                    wait_free(dve, x2_ready, b)
                    nc.vector.scalar_tensor_tensor(hid[:, q, :, :], ez[:], -1.0, z[:], ADD, MAX).then_inc(hid_ready, 1)
                b = it - 3
                if inside(b, BATCH):
                    dve.wait_ge(y_back, b + 1)
                    nc.vector.tensor_tensor(w["x"][:, bass.ds(b * JT, JT), :], pB[:], w["x"][:, bass.ds(b * JT, JT), :], ADD).then_inc(xm_ready, 1)
                b = it - 2
                if inside(b, BATCH):
                    dve.wait_ge(x2_ready, b + 1)
                    wait_free(dve, agg[1], b, per=JT, depth=1)
                    statistics(1, b, par, lambda j: pX[:, j, :])
                b = it - 3
                if inside(b, BATCH):
                    dve.wait_ge(xm_ready, b + 1)
                    wait_free(dve, agg[2], b, per=JT, depth=1)
                    statistics(2, b, q, lambda j: w["x"][:, b * JT + j, :])
                b = it + 1
                if inside(b, BATCH):
                    wait_free(dve, agg[0], b, per=JT, depth=1)
                    statistics(0, b, q, lambda j: w["x1"][:, b * JT + j, :])

            statistics(0, 0, 0, lambda j: w["x1"][:, j, :])
            sweep(dve, BATCH, 5, body, ahead=1)

        @block.gpsimd
        def _(pool):
            def rsigma(i, b, q):
                pool.wait_ge(agg[i], (b + 1) * JT)
                wait_free(pool, rstd[i], b, depth=1)
                wait_free(pool, xn_ready[i], b)
                settle(pool)
                nc.gpsimd.tensor_scalar(ve[i][:], mv[i][:, q, :, 1], EPS[i], None, ADD).then_inc(vard[i], 1)
                pool.wait_ge(vard[i], b + 1)
                nc.gpsimd.tensor_tensor(rs[i][:, q, :], ve[i][:], w["mhalf"][:, 0:JT], ALU.pow).then_inc(rstd[i], 1)

            def body(it, par, pair):
                for i, lag in ((1, 2), (2, 3), (0, -1)):
                    b, q = it - lag, (par - lag) % 2
                    if inside(b, BATCH):
                        rsigma(i, b, q)

            rsigma(0, 0, 0)
            sweep(pool, BATCH, 3, body, ahead=1)

        @block.scalar
        def _(act):
            def body(it, par, pair):
                q = 1 - par
                b = it - 1
                if inside(b, BATCH):
                    act.wait_ge(f1_ready, b + 1)
                    wait_free(act, hid_ready, b, depth=1)
                    for f in range(FC):
                        nc.scalar.activation(z[:, f, :], pF[:, f, :], ACT.Identity, bias=w["b1"][:, f:f + 1]).then_inc(z_ready, 1)
                b = it - 3
                if inside(b, BATCH):
                    act.wait_ge(turned[1], b + 1)
                    wait_free(act, y_back, b, depth=1)
                    nc.scalar.activation(yT[:], pA2[:, 0:SEQ], ACT.Identity, bias=mod[:, b, GAB:GAB + 1], scale=mod[:, b, GAG:GAG + 1]).then_inc(y_ready, 1)
                b = it - 4
                if inside(b, BATCH):
                    act.wait_ge(turned[2], b + 1)
                    wait_free(act, h2_back, b)
                    wait_free(act, h2T_saved, b, per=16)
                    nc.scalar.activation(h2T[:, par, :], pA[:, 0:SEQ], ACT.Identity, bias=mod[:, b, SB:SB + 1], scale=mod[:, b, CB1:CB1 + 1]).then_inc(h2T_ready, 1)
                b = it - 1
                if inside(b, BATCH):
                    act.wait_ge(min_ready, b + 1)
                    nc.scalar.activation(ez[:], ez[:], ACT.Exp).then_inc(e_ready, 1)
                b = it
                if inside(b, BATCH):
                    act.wait_ge(turned[0], b + 1)
                    wait_free(act, x2_ready, b)
                    nc.scalar.activation(o1T[:, par, :], pA[:, 0:SEQ], ACT.Identity, bias=w["ln1"][:, 1:2], scale=w["ln1"][:, 0:1]).then_inc(o1_ready, 1)
                b = it - 4
                if inside(b, BATCH):
                    act.wait_ge(h2_back, b + 1)
                    wait_free(act, cov_ready, b)
                    nc.scalar.activation(h2[:, par, :, 0:D], pXf[:], ACT.Copy).then_inc(h2_ready, 1)

            sweep(act, BATCH, 4, body)

        @block.tensor
        def _(pe):
            pe.wait_ge(init, 2)

            def turn(i, b, dst):
                pe.wait_ge(xn_ready[i], b + 1)
                for j in range(JT):
                    last = nc.tensor.transpose(dst[:, j * P:(j + 1) * P], xn[i][:, j, :], ident[:])
                last.then_inc(turned[i], 1)

            def second(b, par, j):
                if j == 0:
                    pe.wait_ge(hid_ready, b + 1)
                    wait_free(pe, xn_ready[1], b, depth=1)
                tok = slice(j * P, (j + 1) * P)
                for f in range(FC):
                    nc.tensor.matmul(pX[:, j, :], hid[:, par, f, tok], w["w2"][:, f, :], start=(f == 0), stop=False)
                nc.tensor.matmul(pX[:, j, :], w["ones"][0:1, :], w["b2"][0:1, :], start=False, stop=False)
                return nc.tensor.matmul(pX[:, j, :], o1T[:, par, tok], ident[:], start=False, stop=True)

            def body(it, par, pair):
                q = 1 - par
                b = it - 1
                if inside(b, BATCH):
                    pe.wait_ge(o1_ready, b + 1)
                    wait_free(pe, z_ready, b, per=FC, depth=1)
                    for f in range(FC):
                        last = nc.tensor.matmul(pF[:, f, :], w["w1"][:, f * P:(f + 1) * P], o1T[:, q, :], start=True, stop=True)
                    last.then_inc(f1_ready, 1)
                b = it - 3
                if inside(b, BATCH):
                    wait_free(pe, y_ready, b, depth=1)
                    turn(1, b, pA2)
                b = it - 4
                if inside(b, BATCH):
                    if inside(it - 1, BATCH):
                        pe.wait_ge(o1_ready, it)
                    turn(2, b, pA)
                b = it - 5
                if inside(b, BATCH):
                    pe.wait_ge(h2_ready, b + 1)
                    pe.wait_ge(cov_added, b + 1)
                    for j in range(JT):
                        last = nc.tensor.matmul(pC[:], h2[:, q, j, 0:D], h2[:, q, j, :], start=(j == 0), stop=(j == JT - 1))
                    last.then_inc(cov_ready, 1)
                if inside(it - 2, BATCH):
                    second(it - 2, par, 0)
                b = it
                if inside(b, BATCH):
                    if inside(it - 4, BATCH):
                        pe.wait_ge(h2T_ready, it - 3)
                    turn(0, b, pA)
                b = it - 3
                if inside(b, BATCH):
                    pe.wait_ge(y_ready, b + 1)
                    wait_free(pe, xm_ready, b, depth=1)
                    for j in range(JT):
                        last = nc.tensor.transpose(pB[:, j, :], yT[:, j * P:(j + 1) * P], ident[:])
                    last.then_inc(y_back, 1)
                if inside(it - 2, BATCH):
                    second(it - 2, par, 1).then_inc(x2_ready, 1)
                b = it - 4
                if inside(b, BATCH):
                    pe.wait_ge(h2T_ready, b + 1)
                    wait_free(pe, h2_ready, b, depth=1)
                    for j in range(JT):
                        last = nc.tensor.transpose(pXf[:, j, :], h2T[:, par, j * P:(j + 1) * P], ident[:])
                    last.then_inc(h2_back, 1)

            sweep(pe, BATCH, 5, body)

        @block.sync
        def _(sp):
            for dst, src in (
                (w["krow"][:], io["keys"].rearrange("h k a c -> (h k a) c").rearrange("(g r) c -> r g c", r=P)),
                (w["down"][:], io["down"].rearrange("(g e) d -> e g d", e=P)),
                (w["wq"][:], io["w_q"]),
                (w["up"][:], io["up"].rearrange("(g e) d -> e g d", e=P)),
                (w["grow"][:], io["gamma"].rearrange("(g c) -> g c", c=P)),
                (w["brow"][:], io["beta"].rearrange("(g c) -> g c", c=P)),
            ):
                sp.dma_start(dst, src).then_inc(loaded, 16)

            def body(it, par, pair):
                b = it
                if inside(b, BATCH):
                    hold(sp, h2T_ready, b + 1)
                    wait_free(sp, h2T_saved, b, per=16, depth=1)
                    settle(sp)
                    sp.dma_start(w["h2T"][:, b, :], h2T[:, par, :]).then_inc(h2T_saved, 16)

            sweep(sp, BATCH, 0, body)
            sp.wait_ge(h2T_saved, 16 * BATCH)
            sp.wait_ge(loaded, 96)


def fold_phase(nc, w, io):
    with ExitStack() as ctx:
        t = Tools(nc, ctx, "fold")
        wqT = t.sb("wqT", [P, QB, P])
        keysT = t.sb("keysT", [P, PH, NK, 2])
        keysS = t.sb("keysS", [P, QB, NK])
        wq, krow, down, grow, brow = (w[n] for n in ("wq", "krow", "down", "grow", "brow"))
        gT = t.sb("gT", [P, QB])
        bT = t.sb("bT", [P, QB])
        cm = t.sb("cm", [P, D + 1])
        mrow = t.sb("mrow", [1, P])
        prod = t.sb("prod", [P, 3, P])
        var = t.sb("var", [P, QB])
        mean = t.sb("mean", [P, QB])
        var_e = t.sb("var_e", [P, QB])
        inv = t.sb("inv", [P, QB])
        s_ = t.sb("scale", [P, QB])
        sh = t.sb("shift", [P, QB])
        pa = [t.ps(f"pa{i}", [P, 4, P]) for i in range(2)]
        pc = [t.ps(f"pc{i}", [P, 3, D + 1]) for i in range(2)]
        pm = t.ps("pm", [P, 512])
        pw = t.ps("pw", [P, QB, NK])
        pb = t.ps("pb", [1, QB, NK])
        turned, turned_used = t.sem("turned"), t.sem("turned_used")
        vec, m_ready, m_turned, mm_ready, cm_ready = (t.sem(n) for n in ("vec", "m_ready", "m_turned", "mm_ready", "cm_ready"))
        q_ready, q_used, v_ready, ve_ready, pool_done, keys_ready, sh_ready, w_ready = (
            t.sem(n) for n in ("q_ready", "q_used", "v_ready", "ve_ready", "pool_done", "keys_ready", "sh_ready", "w_ready"))
        block = ctx.enter_context(nc.Block())
        ident = w["ident"]
        blocks = [(krow[:, g, :], keysT[:].rearrange("p h k a -> p (h k a)")[:, g * P:(g + 1) * P]) for g in range(4)]
        blocks += [(down[:, g, :], w["downT"][:, g, :]) for g in range(EB)]
        blocks += [(wq[:, g * P:(g + 1) * P], wqT[:, g, :]) for g in range(QB)]
        NB = len(blocks) // 4
        dests = ([keysT[:].rearrange("p h k a -> p (h k a)").rearrange("p (g e) -> p g e", g=4)]
                 + [w["downT"][:, 4 * g:4 * g + 4, :] for g in range(EB // 4)]
                 + [wqT[:, 4 * g:4 * g + 4, :] for g in range(QB // 4)])
        qgroups = [list(range(g, min(g + 3, QB))) for g in range(0, QB, 3)]

        @block.gpsimd
        def _(pool):
            nc.gpsimd.iota(w["iotaE"][:], [[1, P], [0, HALF]], base=0, channel_multiplier=0,
                           allow_small_or_imprecise_dtypes=True).then_inc(pool_done, 1)
            nc.gpsimd.iota(w["iota8"][:], [[1, EB], [0, HALF]], base=0, channel_multiplier=0,
                           allow_small_or_imprecise_dtypes=True).then_inc(pool_done, 1)
            nc.gpsimd.iota(w["order"][:], [[0, PH], [-int(KEYB), CAND]], base=32 * int(KEYB), channel_multiplier=0,
                           allow_small_or_imprecise_dtypes=True).then_inc(pool_done, 1)
            pool.wait_ge(ve_ready, 1)
            nc.gpsimd.tensor_tensor(inv[:], var_e[:], w["mhalf"][:], ALU.pow).then_inc(pool_done, 1)
            pool.wait_ge(pool_done, 4)

        @block.tensor
        def _(pe):
            pe.wait_ge(m_ready, 1)
            nc.tensor.transpose(pm[0:1, 0:P], cm[:, D:D + 1], ident[:]).then_inc(m_turned, 1)
            pe.wait_ge(m_ready, 2)
            nc.tensor.matmul(pm[:, P:2 * P], mrow[:], mrow[:], start=True, stop=True).then_inc(mm_ready, 1)
            pe.wait_ge(cm_ready, 1)
            nc.tensor.transpose(pm[:, 2 * P:2 * P + QB], grow[:], ident[0:QB, 0:QB])
            nc.tensor.transpose(pm[:, 3 * P:3 * P + QB], brow[:], ident[0:QB, 0:QB]).then_inc(mm_ready, 1)
            for k in range(NB):
                if k >= 2:
                    pe.wait_ge(turned_used, k - 1)
                for q in range(4):
                    last = nc.tensor.transpose(pa[k % 2][:, q, :], blocks[4 * k + q][0], ident[:])
                last.then_inc(turned, 1)
            for k, group in enumerate(qgroups):
                if k >= 2:
                    pe.wait_ge(q_used, k - 1)
                for i, g in enumerate(group):
                    last = nc.tensor.matmul(pc[k % 2][:, i, :], wq[:, g * P:(g + 1) * P], cm[:], start=True, stop=True)
                last.then_inc(q_ready, 1)
            pe.wait_ge(turned_used, NB)
            pe.wait_ge(keys_ready, 2)
            for g in range(QB):
                last = nc.tensor.matmul(pw[:, g, :], wqT[:, g, :], keysS[:, g, :], start=True, stop=True)
            last.then_inc(w_ready, 1)
            pe.wait_ge(sh_ready, 1)
            for g in range(QB):
                last = nc.tensor.matmul(pb[:, g, :], sh[:, g:g + 1], keysT[:, g % PH, :, g // PH], start=True, stop=True)
            last.then_inc(w_ready, 1)

        @block.vector
        def _(dve):
            c = Chain(dve, vec)
            n = 1.0 / (BATCH * SEQ)
            nc.vector.tensor_scalar(cm[:, D:D + 1], w["cov"][:, D:D + 1], n, None, MUL).then_inc(m_ready, 1)
            dve.wait_ge(m_turned, 1)
            nc.vector.tensor_copy(mrow[:], pm[0:1, 0:P]).then_inc(m_ready, 1)
            c.link(nc.vector.tensor_scalar(prod[:, 0, :], w["cov"][:, 0:D], n, None, MUL))
            c.wait()
            dve.wait_ge(mm_ready, 1)
            nc.vector.tensor_tensor(cm[:, 0:D], prod[:, 0, :], pm[:, P:2 * P], SUB).then_inc(cm_ready, 1)
            dve.wait_ge(mm_ready, 2)
            c.link(nc.vector.tensor_copy(gT[:], pm[:, 2 * P:2 * P + QB]))
            c.link(nc.vector.tensor_copy(bT[:], pm[:, 3 * P:3 * P + QB]))
            for k in range(NB):
                dve.wait_ge(turned, k + 1)
                nc.vector.tensor_copy(dests[k], pa[k % 2][:]).then_inc(turned_used, 1)
            dve.wait_ge(turned_used, NB)
            dve.wait_ge(cm_ready, 1)
            for k, group in enumerate(qgroups):
                m = len(group)
                g = group[0]
                dve.wait_ge(q_ready, k + 1)
                c.wait()
                c.link(nc.vector.tensor_tensor(prod[:, 0:m, :], pc[k % 2][:, 0:m, 0:D], wqT[:, g:g + m, :], MUL))
                nc.vector.tensor_copy(mean[:, g:g + m], pc[k % 2][:, 0:m, D]).then_inc(q_used, 1)
                c.wait()
                c.link(nc.vector.tensor_reduce(var[:, g:g + m], prod[:, 0:m, :], AX.X, ADD))
            c.wait()
            nc.vector.tensor_scalar(var_e[:], var[:], 0.0, EPS_BN, MAX, ADD).then_inc(ve_ready, 1)
            dve.wait_ge(pool_done, 4)
            c.link(nc.vector.tensor_tensor(s_[:], gT[:], inv[:], MUL))
            c.wait()
            dve.wait_ge(q_used, len(qgroups))
            for a in range(2):
                nc.vector.tensor_tensor(keysS[:, a * PH:(a + 1) * PH, :], keysT[:, :, :, a], bc(s_[:, a * PH:(a + 1) * PH], 2, NK),
                                        MUL).then_inc(keys_ready, 1)
            c.link(nc.vector.tensor_tensor(mean[:], mean[:], s_[:], MUL))
            c.wait()
            nc.vector.tensor_tensor(sh[:], bT[:], mean[:], SUB).then_inc(sh_ready, 1)
            dve.wait_ge(w_ready, 2)
            nc.vector.tensor_copy(w["wkey"][:], pw[:].rearrange("p g k -> p (g k)"))
            nc.vector.tensor_copy(w["bkey"][:], pb[:].rearrange("p g k -> p (g k)"))


def experts_phase(nc, w, out):
    with ExitStack() as ctx:
        t = Tools(nc, ctx, "exp")
        C8 = CAND + TOPK
        h2c = t.sb("h2c", [P, 2, P])
        sims = t.sb("sims", [P, 2, QB, NK])
        sv = t.sb("sv", [P, QB, TOPK])
        si = t.sb("si", [P, 2, QB, TOPK], U16)
        row = t.sb("row", [P, PH, TOPK])
        col = t.sb("col", [P, PH, TOPK])
        cand = t.sb("cand", [P, PH, C8])
        over = t.sb("over", [P, PH, CAND])
        ge = t.sb("ge", [P, PH, CAND])
        rel = t.sb("rel", [P, 2, PH, C8])
        place = t.sb("place", [P, PH, CAND])
        pay = t.sb("pay", [P, 3, PH, CAND])
        zsum = t.sb("zsum", [P, 2, PH])
        rz = t.sb("rz", [P, 2, PH])
        wt = t.sb("wt", [P, PH, CAND])
        wr = t.sb("wr", [P, PH, CAND])
        keyv = t.sb("keyv", [P, 2, 3, PH, CAND])
        kept = t.sb("kept", [P, 3, PH, TOPK], U32)
        bits = t.sb("bits", [P, 4, PAIR], U32)
        half = t.sb("half", [P, 4, 2, PAIR], F16)
        pairs = t.sb("pairs", [P, 2, 4, HALF], F16)
        onee = t.sb("onee", [P, P, HALF], F16)
        oneb = t.sb("oneb", [P, EB, HALF], F16)
        wb = t.sb("wb", [P, 2, EB, 2, HALF], F16)
        act_e = t.sb("act_e", [P, EB, P])
        prod = t.sb("prod", [P, EB, P])
        yT = t.sb("yT", [P, P])
        xo = t.sb("xo", [P, 2, D])
        pS = t.ps("pS", [P, QB, NK])
        pT = t.ps("pT", [P, 4, P], F16)
        pW = [t.ps(f"pW{i}", [P, HALF // 2, EB, 2]) for i in range(2)]
        pG = t.ps("pG", [P, EB, P])
        pO = t.ps("pO", [P, 512])
        pF = t.ps("pF", [P, 512])
        h2_loaded = [t.sem(f"h2_loaded{i}") for i in range(2)]
        stored = [t.sem(f"stored{i}") for i in range(2)]
        names = ("sims_ready sims_kept best index cand_sum best8 flags rel_ready sum_ready rz_ready exp_ready rc_ready "
                 "pay_w pay_i place_ready keys_made packed masked half_ready turned pairs_ready one_ready oneb_ready wb_ready "
                 "w_ready g_ready gelu_ready prod_ready o_ready y_ready back xo_ready init steps").split()
        S = {n: t.sem(n) for n in names}
        block = ctx.enter_context(nc.Block())
        ident, ident16, mod = w["ident"], w["ident16"], w["mod"]
        starts = [sum(RANKS[:a]) for a in range(TOPK)]

        @block.sync
        def _(sp):
            o = out.rearrange("b (j p) d -> b j p d", p=P)

            def body(it, par, pair):
                n = it
                if inside(n, TILES):
                    wait_free(sp, S["sims_ready"], n)
                    sp.dma_start(h2c[:, par, :], w["h2T"][:, pair, par * P:(par + 1) * P]).then_inc(h2_loaded[par], 16)
                n = it - 6
                if inside(n, TILES):
                    hold(sp, S["xo_ready"], n + 1)
                    sp.dma_start(o[pair - 3, par, :, :], xo[:, par, :]).then_inc(stored[par], 16)

            sweep(sp, TILES, 6, body)
            for p in range(2):
                sp.wait_ge(stored[p], 16 * (TILES // 2))

        @block.vector
        def _(dve):
            V = nc.vector
            V.memset(wb[:], 0.0).then_inc(S["init"], 1)
            dve.wait_ge(S["init"], 1)

            def sums(add, dst, sx, sy, sem):
                s = starts
                add(dst[:, :, 0:8], bc(sx[:, :, 0], 2, 8), sy[:, :, 0:8], ADD).then_inc(sem, 1)
                add(dst[:, :, s[1]:s[1] + 4], bc(sx[:, :, 1], 2, 4), sy[:, :, 0:4], ADD).then_inc(sem, 1)
                add(dst[:, :, s[2]:s[4]].rearrange("p h (a b) -> p h a b", b=2), bc(sx[:, :, 2:4], 3, 2), bc(sy[:, :, 0:2], 2, 2),
                    ADD).then_inc(sem, 1)
                add(dst[:, :, s[4]:s[4] + 4], sx[:, :, 4:8], bc(sy[:, :, 0], 2, 4), ADD).then_inc(sem, 1)

            def body(it, par, pair):
                q = 1 - par
                n = it
                if inside(n, TILES):
                    dve.wait_ge(S["sims_kept"], n + 1)
                    wait_free(dve, S["cand_sum"], n, per=4, depth=1)
                    wait_free(dve, S["index"], n, per=QB, depth=1)
                    settle(dve)
                    for g in range(QB):
                        V.max(sv[:, g, :], sims[:, par, g, :]).then_inc(S["best"], 1)
                n = it - 1
                if inside(n, TILES):
                    dve.wait_ge(S["exp_ready"], n + 1)
                    wait_free(dve, S["pay_w"], n)
                    V.tensor_reduce(zsum[:, q, :], rel[:, q, :, CAND:C8], AX.X, ADD).then_inc(S["sum_ready"], 1)
                n = it
                if inside(n, TILES):
                    wait_free(dve, S["rel_ready"], n, per=2, depth=1)
                    dve.wait_ge(S["best"], (n + 1) * QB)
                    sums(V.tensor_tensor, cand, sv[:, 0:PH, :], sv[:, PH:QB, :], S["cand_sum"])
                n = it - 1
                if inside(n, TILES):
                    dve.wait_ge(S["sum_ready"], n + 1)
                    V.reciprocal(rz[:, q, :], zsum[:, q, :]).then_inc(S["rz_ready"], 1)
                n = it
                if inside(n, TILES):
                    wait_free(dve, S["rc_ready"], n, per=2)
                    settle(dve)
                    for g in range(QB):
                        V.max_index(si[:, par, g, :], sv[:, g, :], sims[:, par, g, :]).then_inc(S["index"], 1)
                    hold(dve, S["cand_sum"], (n + 1) * 4)
                    for h in range(PH):
                        V.max(cand[:, h, CAND:C8], cand[:, h, 0:CAND]).then_inc(S["best8"], 1)
                n = it - 4
                if inside(n, TILES):
                    dve.wait_ge(S["gelu_ready"], n + 1)
                    dve.wait_ge(S["w_ready"], n * 2 + 2)
                    wait_free(dve, S["o_ready"], n, depth=1)
                    for i in range(2):
                        tok = slice(i * HALF, (i + 1) * HALF)
                        V.tensor_tensor(prod[:, :, tok].rearrange("p e (t a) -> p e t a", a=2),
                                        pW[i][:].rearrange("p t e a -> p e t a"),
                                        act_e[:, :, tok].rearrange("p e (t a) -> p e t a", a=2), MUL).then_inc(S["prod_ready"], 1)
                n = it - 2
                if inside(n, TILES):
                    dve.wait_ge(S["keys_made"], n + 1)
                    wait_free(dve, S["masked"], n, per=3, depth=1)
                    settle(dve)
                    for f in range(3):
                        for h in range(PH):
                            V.max(kept[:, f, h, :], keyv[:, par, f, h, :]).then_inc(S["packed"], 1)
                n = it - 3
                if inside(n, TILES):
                    v = pairs[:, q, :, :]
                    dve.wait_ge(S["pairs_ready"], (n + 1) * 2)
                    wait_free(dve, S["w_ready"], n, per=2, depth=1)
                    wait_free(dve, S["wb_ready"], n, per=2, depth=1)
                    V.tensor_tensor(oneb[:], bc(v[:, 1, :], 1, EB), w["iota8"][:], ALU.is_equal).then_inc(S["oneb_ready"], 1)
                n = it - 2
                if inside(n, TILES):
                    wait_free(dve, S["half_ready"], n, per=2, depth=1)
                    dve.wait_ge(S["packed"], (n + 1) * 3 * PH)
                    flat = kept[:].rearrange("p f h k -> p f (h k)")
                    V.tensor_scalar(bits[:, 0, :], flat[:, 0, :], P - 1, None, ALU.bitwise_and).then_inc(S["masked"], 1)
                    V.tensor_scalar(bits[:, 1, :], flat[:, 0, :], 7, EB - 1, ALU.logical_shift_right, ALU.bitwise_and).then_inc(S["masked"], 1)
                    V.tensor_scalar(bits[:, 2:4, :], flat[:, 1:3, :], int(KEYB) - 1, None, ALU.bitwise_and).then_inc(S["masked"], 1)
                n = it - 3
                if inside(n, TILES):
                    V.tensor_tensor(onee[:], bc(v[:, 0, :], 1, P), w["iotaE"][:], ALU.is_equal).then_inc(S["one_ready"], 1)
                    dve.wait_ge(S["oneb_ready"], n + 1)
                    for a in range(2):
                        r = slice(a * PAIR, (a + 1) * PAIR)
                        V.tensor_tensor(wb[r, :, :, a, :], bc(oneb[r, :, :], 1, 2), bc(v[r, 2:4, :], 2, EB), MUL).then_inc(S["wb_ready"], 1)

            sweep(dve, TILES, 4, body)

        @block.gpsimd
        def _(pool):
            G = nc.gpsimd

            def body(it, par, pair):
                q = 1 - par
                n = it - 1
                if inside(n, TILES):
                    hold(pool, S["index"], (n + 1) * QB)
                    G.tensor_scalar(row[:], si[:, q, 0:PH, :], float(NK), None, MUL).then_inc(S["rc_ready"], 1)
                    G.tensor_scalar(col[:], si[:, q, PH:QB, :], 1.0, None, MUL).then_inc(S["rc_ready"], 1)
                    pool.wait_ge(S["rc_ready"], (n + 1) * 2)
                    s = starts
                    i_ = pay[:, 0, :, :]
                    wait_free(pool, S["keys_made"], n, depth=1)
                    G.tensor_tensor(i_[:, :, 0:8], bc(row[:, :, 0], 2, 8), col[:, :, 0:8], ADD).then_inc(S["pay_i"], 1)
                    G.tensor_tensor(i_[:, :, s[1]:s[1] + 4], bc(row[:, :, 1], 2, 4), col[:, :, 0:4], ADD).then_inc(S["pay_i"], 1)
                    G.tensor_tensor(i_[:, :, s[2]:s[2] + 2], bc(row[:, :, 2], 2, 2), col[:, :, 0:2], ADD).then_inc(S["pay_i"], 1)
                    G.tensor_tensor(i_[:, :, s[3]:s[3] + 2], bc(row[:, :, 3], 2, 2), col[:, :, 0:2], ADD).then_inc(S["pay_i"], 1)
                    G.tensor_tensor(i_[:, :, s[4]:s[4] + 4], row[:, :, 4:8], bc(col[:, :, 0], 2, 4), ADD).then_inc(S["pay_i"], 1)
                    c = Chain(pool, S["steps"], n * 5)
                    pool.wait_ge(S["rz_ready"], n + 1)
                    G.tensor_tensor(wt[:], rel[:, q, :, 0:CAND], bc(rz[:, q, :], 2, CAND), MUL).then_inc(S["pay_w"], 1)
                    hold(pool, S["pay_w"], n + 1)
                    c.link(G.tensor_scalar(wr[:], wt[:], WSCALE, RND, MUL, ADD))
                    c.link(G.tensor_scalar(wt[:], wt[:], WSCALE, None, MUL))
                    c.wait()
                    c.link(G.tensor_scalar(pay[:, 1, :, :], wr[:], RND, None, SUB))
                    c.wait()
                    c.link(G.tensor_tensor(wt[:], wt[:], pay[:, 1, :, :], SUB))
                    c.wait()
                    c.link(G.tensor_scalar(pay[:, 2, :, :], wt[:], 2 * WSCALE, WSCALE, MUL, ADD))
                    c.wait()
                    assert c.k == 5
                    pool.wait_ge(S["place_ready"], n + 1)
                    pool.wait_ge(S["pay_i"], (n + 1) * 5)
                    wait_free(pool, S["packed"], n, per=3 * PH)
                    G.tensor_tensor(keyv[:, q, :, :, :].rearrange("p f h c -> p f (h c)"), pay[:].rearrange("p f h c -> p f (h c)"),
                                    bc(place[:].rearrange("p h c -> p (h c)"), 1, 3), ADD).then_inc(S["keys_made"], 1)
                n = it
                if inside(n, TILES):
                    pool.wait_ge(S["best8"], (n + 1) * PH)
                    wait_free(pool, S["pay_w"], n)
                    G.tensor_tensor(rel[:, par, :, :], cand[:], bc(cand[:, :, CAND], 2, C8), SUB).then_inc(S["rel_ready"], 1)
                    G.tensor_tensor(over[:], cand[:, :, 0:CAND], bc(cand[:, :, C8 - 1], 2, CAND), SUB).then_inc(S["rel_ready"], 1)
                    hold(pool, S["rel_ready"], (n + 1) * 2)
                    G.tensor_scalar(place[:], over[:], 0.0, 32 * KEYB, ALU.is_gt, MUL).then_inc(S["flags"], 1)
                    G.tensor_scalar(ge[:], over[:], 0.0, None, ALU.is_ge).then_inc(S["flags"], 1)
                    pool.wait_ge(S["flags"], n * 3 + 2)
                    G.tensor_tensor(place[:], place[:], w["order"][:], ADD).then_inc(S["flags"], 1)
                    pool.wait_ge(S["flags"], n * 3 + 3)
                    G.tensor_tensor(place[:], place[:], ge[:], MUL).then_inc(S["place_ready"], 1)

            sweep(pool, TILES, 1, body)

        @block.scalar
        def _(act):
            A = nc.scalar.activation

            def keep_sims(n, q):
                act.wait_ge(S["sims_ready"], n + 1)
                wait_free(act, S["index"], n, per=QB)
                A(sims[:, q, :, :], pS[:], ACT.Copy).then_inc(S["sims_kept"], 1)

            def body(it, par, pair):
                q = 1 - par
                n = it + 1
                if inside(n, TILES):
                    keep_sims(n, q)
                n = it - 2
                if inside(n, TILES):
                    act.wait_ge(S["masked"], (n + 1) * 3)
                    wait_free(act, S["turned"], n, depth=1)
                    A(half[:, 0:3, :, :].rearrange("p f d k -> p f d k"), bc(bits[:, 0:3, :], 2, 2), ACT.Copy).then_inc(S["half_ready"], 1)
                    A(half[:, 3, :, :], bc(bits[:, 3, :], 1, 2), ACT.Copy, bias=-0.5, scale=0.5 / WSCALE).then_inc(S["half_ready"], 1)
                n = it - 4
                if inside(n, TILES):
                    act.wait_ge(S["o_ready"], n + 1)
                    wait_free(act, S["back"], n, depth=1)
                    settle(act)
                    b = pair - 2
                    A(yT[:], pO[:, 0:P], ACT.Copy, scale=mod[:, b, GB:GB + 1]).then_inc(S["y_ready"], 1)
                n = it - 2
                if inside(n, TILES):
                    act.wait_ge(S["turned"], n + 1)
                    wait_free(act, S["one_ready"], n)
                    wait_free(act, S["wb_ready"], n, per=2)
                    for a in range(2):
                        r = slice(a * PAIR, (a + 1) * PAIR)
                        A(pairs[r, par, :, :], pT[r, :, :].rearrange("p f (t a) -> p a f t", a=2)[:, a, :, :], ACT.Copy).then_inc(S["pairs_ready"], 1)
                n = it - 5
                if inside(n, TILES):
                    act.wait_ge(S["back"], n + 1)
                    if not isinstance(n, int) or n >= 2:
                        act.wait_ge(stored[q], (pair - 3 + par) * 16)
                    A(xo[:, q, :], pF[:, 0:D], ACT.Copy).then_inc(S["xo_ready"], 1)
                n = it
                if inside(n, TILES):
                    act.wait_ge(S["rel_ready"], n * 2 + 1)
                    A(rel[:, par, :, :], rel[:, par, :, :], ACT.Exp).then_inc(S["exp_ready"], 1)
                n = it - 3
                if inside(n, TILES):
                    act.wait_ge(S["g_ready"], n + 1)
                    wait_free(act, S["prod_ready"], n, per=2, depth=1)
                    A(act_e[:], pG[:], ACT.Gelu_apprx_tanh).then_inc(S["gelu_ready"], 1)

            keep_sims(0, 0)
            sweep(act, TILES, 5, body, ahead=1)

        @block.tensor
        def _(pe):
            def scores(n, q, count):
                pe.wait_ge(h2_loaded[q], count * 16)
                wait_free(pe, S["sims_kept"], n, depth=1)
                nc.tensor.matmul(pS[:].rearrange("p g k -> p (g k)"), h2c[:, q, :], w["wkey"][:], start=True, stop=False)
                nc.tensor.matmul(pS[:].rearrange("p g k -> p (g k)"), w["ones"][0:1, :], w["bkey"][:], start=False, stop=True).then_inc(S["sims_ready"], 1)

            def body(it, par, pair):
                n = it - 5
                if inside(n, TILES):
                    pe.wait_ge(S["y_ready"], n + 1)
                    wait_free(pe, S["xo_ready"], n, depth=1)
                    nc.tensor.matmul(pF[:, 0:D], yT[:], ident[:], start=True, stop=False)
                    nc.tensor.matmul(pF[:, 0:D], ident[:], w["x"][:, n, :], start=False, stop=True).then_inc(S["back"], 1)
                n = it + 1
                if inside(n, TILES):
                    scores(n, 1 - par, pair + 1 + par)
                n = it - 3
                if inside(n, TILES):
                    wait_free(pe, S["gelu_ready"], n, depth=1)
                    b, j = (pair - 2, 1) if par == 0 else (pair - 1, 0)
                    for e in range(EB):
                        last = nc.tensor.matmul(pG[:, e, :], w["downT"][:, e, :], w["h2T"][:, b, j * P:(j + 1) * P], start=True, stop=True)
                    last.then_inc(S["g_ready"], 1)
                n = it - 4
                if inside(n, TILES):
                    pe.wait_ge(S["prod_ready"], (n + 1) * 2)
                    wait_free(pe, S["y_ready"], n, depth=1)
                    for e in range(EB):
                        last = nc.tensor.matmul(pO[:, 0:P], w["up"][:, e, :], prod[:, e, :], start=(e == 0), stop=(e == EB - 1))
                    last.then_inc(S["o_ready"], 1)
                n = it - 2
                if inside(n, TILES):
                    pe.wait_ge(S["half_ready"], (n + 1) * 2)
                    wait_free(pe, S["pairs_ready"], n, per=2, depth=1)
                    for f in range(4):
                        last = nc.tensor.transpose(pT[:, f, :], half[:, f, :, :].rearrange("p d k -> p (d k)"), ident16[:])
                    last.then_inc(S["turned"], 1)
                n = it - 3
                if inside(n, TILES):
                    pe.wait_ge(S["one_ready"], n + 1)
                    pe.wait_ge(S["wb_ready"], (n + 1) * 2)
                    wait_free(pe, S["prod_ready"], n, per=2, depth=1)
                    for i in range(2):
                        for k in range(HALF // 2):
                            p = i * (HALF // 2) + k
                            for part in range(2):
                                last = nc.tensor.matmul(pW[i][:, k, :, :].rearrange("p e a -> p (e a)"), onee[:, :, p],
                                                        wb[:, part, :, :, p].rearrange("p e a -> p (e a)"),
                                                        start=(part == 0), stop=(part == 1))
                        last.then_inc(S["w_ready"], 1)

            scores(0, 0, 1)
            sweep(pe, TILES, 5, body, ahead=1)


def build(nc, io, out):
    with ExitStack() as ctx:
        t = Tools(nc, ctx, "w")
        w = {}
        for name, shape, dt in (
            ("ident", [P, P], F32), ("ident16", [P, P], F16), ("ones", [P, P], F32), ("mhalf", [P, QB], F32), ("x1", [P, TILES, D], F32),
            ("x", [P, TILES, D], F32), ("mod", [P, BATCH, NV], F32),
            ("w1", [P, DFF], F32), ("w2", [P, FC, D], F32), ("b1", [P, FC], F32), ("b2", [1, D], F32), ("ln1", [P, 2], F32),
        ):
            w[name] = t.sb(name, shape, dt)
        with ExitStack() as ctx2:
            t2 = Tools(nc, ctx2, "w")
            for name, shape in (
                ("hT", [P, BATCH, SEQ]), ("G", [P, BATCH, HM]), ("ksum", [P, BATCH, PAIRS]), ("hsum", [P, BATCH]), ("cmax", [P, BATCH]),
                ("WqP", [P, HM]), ("WkP", [P, HM]), ("Wvo", [P, HEADS * D]), ("Wq", [P, HM]), ("Wk", [P, HM]),
            ):
                w[name] = t2.sb(name, shape)
            setup(nc, w, io)
            keys_phase(nc, w, io)
            queries_phase(nc, w)
        with ExitStack() as ctx2:
            t2 = Tools(nc, ctx2, "w")
            for name, shape in (
                ("h2T", [P, BATCH, SEQ]), ("cov", [P, D + 1]), ("up", [P, EB, D]), ("down", [P, EB, P]), ("krow", [P, 4, P]),
                ("wq", [P, QB * P]), ("grow", [QB, P]), ("brow", [QB, P]),
            ):
                w[name] = t2.sb(name, shape)
            ffn_phase(nc, w, io)
            for name, shape, dt in (
                ("downT", [P, EB, P], F32), ("wkey", [P, QB * NK], F32), ("bkey", [1, QB * NK], F32),
                ("iotaE", [P, P, HALF], F16), ("iota8", [P, EB, HALF], F16), ("order", [P, PH, CAND], F32),
            ):
                w[name] = t2.sb(name, shape, dt)
            fold_phase(nc, w, io)
            experts_phase(nc, w, out)


_NAMES = {
    "x": "L0_attn_x", "Wq": "L0_attn_Wq", "Wk": "L0_attn_Wk", "Wv": "L0_attn_Wv", "Wo": "L0_attn_Wo", "proj": "L0_attn_proj",
    "W1": "L0_attn_W1", "b1": "L0_attn_b1", "W2": "L0_attn_W2", "b2": "L0_attn_b2",
    "ln1_g": "L0_attn_ln1_g", "ln1_b": "L0_attn_ln1_b", "ln2_g": "L0_attn_ln2_g", "ln2_b": "L0_attn_ln2_b",
    "w_q": "L0_ffn_w_q", "gamma": "L0_ffn_bn_gamma", "beta": "L0_ffn_bn_beta", "keys": "L0_ffn_keys",
    "down": "L0_ffn_down_embed", "up": "L0_ffn_up_embed", "c": "L0_c", "wmod": "L0_wmod",
}


def kernel(**inputs):
    import numpy as _np
    import concourse.bacc as _bacc
    from concourse import mybir as _mybir
    from concourse.bass_utils import run_bass_kernel_spmd as _run

    nc = _bacc.Bacc("TRN2", target_bir_lowering=False, num_devices=1)
    arrays, io = {}, {}
    for short, name in _NAMES.items():
        a = _np.ascontiguousarray(inputs[name])
        arrays[f"in_{name}"] = a
        io[short] = nc.dram_tensor(f"in_{name}", a.shape, _mybir.dt.from_np(a.dtype), kind="ExternalInput").ap()
    out = nc.dram_tensor("out", (BATCH, SEQ, D), _mybir.dt.float32, kind="ExternalOutput").ap()
    build(nc, io, out)
    return _run(nc, [arrays], core_ids=[0]).results[0]["out"]
```
